# Optimizing a Trainium2 kernel written in Bass

```python
import numpy as np
import jax
import jax.numpy as jnp

def _softmax(x, axis=-1):
    return jax.nn.softmax(x, axis=axis)

def _gelu(x):
    return jax.nn.gelu(x, approximate=True)

def _silu(x):
    return jax.nn.silu(x)

def _sigmoid(x):
    return jax.nn.sigmoid(x)

def _layernorm(x, axis=-1, eps=1e-05):
    m = jnp.mean(x, axis=axis, keepdims=True)
    v = jnp.var(x, axis=axis, keepdims=True)
    return (x - m) / jnp.sqrt(v + eps)

def _scatter_add(tgt, idx, src, axis=0):
    return tgt.at[idx].add(src)

def _segment_sum(src, seg, n):
    return jax.ops.segment_sum(src, seg, n)
kernel_name = 'mk_lm_tower_d1_tok_ids256_r4_cce5fc'

def setup_inputs(seed: int=0):
    np.random.seed(seed)
    _w = jnp.asarray

    def _rec_inputs():
        import jax
        import jax.numpy as jnp
        _rk = jax.random.key(seed)
        x = jax.random.randint(jax.random.fold_in(_rk, 1), (128, 128), 0, 250, jnp.int32)
        return x
    x = _rec_inputs()

    def _L0_tok_setup():
        import jax, jax.numpy as jnp
        import numpy as np
        B, T, H, VOCAB = (128, 128, 64, 250)
        EPS = 1e-12

        def _pos_graph(seq_inputs):
            si = seq_inputs[:, :, None]
            mask = si != 0
            equal = si == si.transpose(0, 2, 1)
            tril = jnp.tril(jnp.ones((si.shape[1], si.shape[1]), dtype=jnp.float32))
            rel = equal.astype(jnp.float32) * tril
            rel = rel * mask.astype(jnp.float32) * mask.transpose(0, 2, 1).astype(jnp.float32)
            norm = rel.sum(-2, keepdims=True)
            norm = jnp.where(norm == 0, 1.0, norm)
            return rel / norm

        def _get_pos_emb(seq_inputs, emb_table):
            seq_mask = seq_inputs != 0
            length = seq_mask.sum(1, keepdims=True)
            coo = jnp.arange(seq_inputs.shape[1])[None, :] * seq_mask
            pos_index = (length - coo) * seq_mask
            return emb_table[pos_index]
        key = jax.random.key(seed)
        k1, k2, k3, k4 = jax.random.split(key, 4)
        stdv = 1.0 / np.sqrt(H)
        seq_inputs = jax.random.randint(k1, (B, T), 0, VOCAB, dtype=jnp.int64 if jax.config.jax_enable_x64 else jnp.int32)
        emb_table = jax.random.normal(k2, (T + 1, H), dtype=jnp.float32)
        W_in = jax.random.uniform(k3, (H, H), minval=-stdv, maxval=stdv, dtype=jnp.float32)
        b_oah = jax.random.uniform(k4, (H,), minval=-stdv, maxval=stdv, dtype=jnp.float32)
        return {'seq_inputs': seq_inputs, 'emb_table': emb_table, 'W_in': W_in, 'b_oah': b_oah}
    _L0_tok_all = _L0_tok_setup()
    _L0_tok_in = {k: v for k, v in _L0_tok_all.items() if k in ('emb_table', 'W_in', 'b_oah')}
    del _L0_tok_all

    def _L0_attn_setup():
        import jax, jax.numpy as jnp
        import numpy as np
        DIM = 64
        HEADS = 4
        DIM_HEAD = 64
        INNER = HEADS * DIM_HEAD
        SCALE = DIM_HEAD ** (-0.5)
        key = jax.random.key(seed)
        k1, k2, k3 = jax.random.split(key, 3)
        x = jax.random.normal(k1, (4, 1024, DIM), dtype=jnp.float32)
        w_qkv = jax.random.normal(k2, (3 * INNER, DIM), dtype=jnp.float32) * DIM ** (-0.5)
        w_out = jax.random.normal(k3, (DIM, INNER), dtype=jnp.float32) * INNER ** (-0.5)
        b_out = jnp.zeros((DIM,), dtype=jnp.float32)
        return {'x': x, 'w_qkv': w_qkv, 'w_out': w_out, 'b_out': b_out}
    _L0_attn_all = _L0_attn_setup()
    _L0_attn_in = {k: v for k, v in _L0_attn_all.items() if k in ('w_qkv', 'w_out', 'b_out')}
    del _L0_attn_all

    def _L0_ffn_setup():
        import jax, jax.numpy as jnp
        import numpy as np
        E = 8
        K = 2
        D = 64
        H = 128
        DOUT = 64
        EPS = 1e-05
        key = jax.random.key(seed)
        ks = jax.random.split(key, 9)
        s = 0.02
        return {'x': jax.random.normal(ks[0], (4, 2048, D), jnp.float32), 'gamma': 1.0 + 0.05 * jax.random.normal(ks[1], (D,), jnp.float32), 'beta': 0.05 * jax.random.normal(ks[2], (D,), jnp.float32), 'Wr': 0.01 * jax.random.normal(ks[3], (D, E), jnp.float32), 'br': jnp.zeros((E,), jnp.float32), 'W1': s * jax.random.normal(ks[4], (E, D, H), jnp.float32), 'b1': s * jax.random.normal(ks[5], (E, H), jnp.float32), 'W2': s * jax.random.normal(ks[6], (E, H, DOUT), jnp.float32), 'b2': s * jax.random.normal(ks[7], (E, DOUT), jnp.float32)}
    _L0_ffn_all = _L0_ffn_setup()
    _L0_ffn_in = {k: v for k, v in _L0_ffn_all.items() if k in ('gamma', 'beta', 'Wr', 'br', 'W1', 'b1', 'W2', 'b2')}
    del _L0_ffn_all
    return {'x': x, 'L0_tok_emb_table': _L0_tok_in['emb_table'], 'L0_tok_W_in': _L0_tok_in['W_in'], 'L0_tok_b_oah': _L0_tok_in['b_oah'], 'L0_attn_w_qkv': _L0_attn_in['w_qkv'], 'L0_attn_w_out': _L0_attn_in['w_out'], 'L0_attn_b_out': _L0_attn_in['b_out'], 'L0_ffn_gamma': _L0_ffn_in['gamma'], 'L0_ffn_beta': _L0_ffn_in['beta'], 'L0_ffn_Wr': _L0_ffn_in['Wr'], 'L0_ffn_br': _L0_ffn_in['br'], 'L0_ffn_W1': _L0_ffn_in['W1'], 'L0_ffn_b1': _L0_ffn_in['b1'], 'L0_ffn_W2': _L0_ffn_in['W2'], 'L0_ffn_b2': _L0_ffn_in['b2']}

def reference(x, L0_tok_emb_table, L0_tok_W_in, L0_tok_b_oah, L0_attn_w_qkv, L0_attn_w_out, L0_attn_b_out, L0_ffn_gamma, L0_ffn_beta, L0_ffn_Wr, L0_ffn_br, L0_ffn_W1, L0_ffn_b1, L0_ffn_W2, L0_ffn_b2):
    import jax
    import jax.numpy as jnp

    def _L0_tok_ref(seq_inputs, emb_table, W_in, b_oah):
        import jax, jax.numpy as jnp
        import numpy as np
        B, T, H, VOCAB = (128, 128, 64, 250)
        EPS = 1e-12

        def _pos_graph(seq_inputs):
            si = seq_inputs[:, :, None]
            mask = si != 0
            equal = si == si.transpose(0, 2, 1)
            tril = jnp.tril(jnp.ones((si.shape[1], si.shape[1]), dtype=jnp.float32))
            rel = equal.astype(jnp.float32) * tril
            rel = rel * mask.astype(jnp.float32) * mask.transpose(0, 2, 1).astype(jnp.float32)
            norm = rel.sum(-2, keepdims=True)
            norm = jnp.where(norm == 0, 1.0, norm)
            return rel / norm

        def _get_pos_emb(seq_inputs, emb_table):
            seq_mask = seq_inputs != 0
            length = seq_mask.sum(1, keepdims=True)
            coo = jnp.arange(seq_inputs.shape[1])[None, :] * seq_mask
            pos_index = (length - coo) * seq_mask
            return emb_table[pos_index]
        step = 1
        A_in = _pos_graph(seq_inputs)
        pe = _get_pos_emb(seq_inputs, emb_table)
        nrm = jnp.sqrt(jnp.sum(pe * pe, axis=1, keepdims=True))
        pe = pe / jnp.maximum(nrm, EPS)
        for _ in range(step):
            h_n = jnp.einsum('bth,oh->bto', pe, W_in)
            pe = jnp.einsum('bji,bjh->bih', A_in, h_n) + b_oah
        return pe

    def _L0_attn_ref(x, w_qkv, w_out, b_out):
        import jax, jax.numpy as jnp
        import numpy as np
        DIM = 64
        HEADS = 4
        DIM_HEAD = 64
        INNER = HEADS * DIM_HEAD
        SCALE = DIM_HEAD ** (-0.5)
        b, n, _ = x.shape
        qkv = x @ w_qkv.T
        q, k, v = jnp.split(qkv, 3, axis=-1)

        def heads(t):
            return t.reshape(b, n, HEADS, DIM_HEAD).transpose(0, 2, 1, 3)
        q, k, v = (heads(q), heads(k), heads(v))
        dots = jnp.einsum('bhid,bhjd->bhij', q, k) * SCALE
        attn = jax.nn.softmax(dots, axis=-1)
        out = jnp.einsum('bhij,bhjd->bhid', attn, v)
        out = out.transpose(0, 2, 1, 3).reshape(b, n, INNER)
        return out @ w_out.T + b_out

    def _L0_ffn_ref(x, gamma, beta, Wr, br, W1, b1, W2, b2):
        import jax, jax.numpy as jnp
        import numpy as np
        E = 8
        K = 2
        D = 64
        H = 128
        DOUT = 64
        EPS = 1e-05
        mu = jnp.mean(x, axis=-1, keepdims=True)
        var = jnp.mean(jnp.square(x - mu), axis=-1, keepdims=True)
        xn = (x - mu) * jax.lax.rsqrt(var + EPS) * gamma + beta
        logits = jnp.einsum('bsd,de->bse', xn, Wr) + br
        top_vals, top_idx = jax.lax.top_k(logits, K)
        w = jax.nn.softmax(top_vals, axis=-1)
        w_full = jnp.einsum('bsk,bske->bse', w, jax.nn.one_hot(top_idx, E, dtype=w.dtype))
        y = jnp.zeros(x.shape[:-1] + (DOUT,), x.dtype)
        for e in range(E):
            h = jax.nn.gelu(jnp.einsum('bsd,dh->bsh', xn, W1[e]) + b1[e], approximate=False)
            y_e = jnp.einsum('bsh,hd->bsd', h, W2[e]) + b2[e]
            y = y + y_e * w_full[..., e, None]
        return y
    h = _L0_tok_ref(x, L0_tok_emb_table, L0_tok_W_in, L0_tok_b_oah)
    h = h + _L0_attn_ref(_layernorm(h, axis=-1), L0_attn_w_qkv, L0_attn_w_out, L0_attn_b_out)
    h = h + _L0_ffn_ref(_layernorm(h, axis=-1), L0_ffn_gamma, L0_ffn_beta, L0_ffn_Wr, L0_ffn_br, L0_ffn_W1, L0_ffn_b1, L0_ffn_W2, L0_ffn_b2)
    return h

_drawn_inputs = setup_inputs


def setup_inputs(seed=0):
    import zlib

    import numpy as np

    out = dict(_drawn_inputs(seed))
    spreads = {'L0_attn_b_out': (0.0, 0.1), 'L0_ffn_br': (0.0, 0.1)}
    factors = {'L0_ffn_gamma': 8.0,
     'L0_ffn_beta': 8.0,
     'L0_ffn_Wr': 8.0,
     'L0_ffn_W1': 3.601,
     'L0_ffn_b1': 8.0,
     'L0_ffn_W2': 3.435,
     'L0_ffn_b2': 3.709}
    for name, (base, spread) in spreads.items():
        noise = np.random.default_rng([zlib.crc32(name.encode()), seed]).standard_normal(out[name].shape)
        drawn = base * np.exp(spread * noise) if base else spread * noise
        out[name] = jnp.asarray(drawn.astype(out[name].dtype))
    for name, factor in factors.items():
        out[name] = (out[name] * factor).astype(out[name].dtype)
    return out
```

```python
from contextlib import ExitStack

import concourse.bass as bass
from concourse import mybir

F32 = mybir.dt.float32
F32R = mybir.dt.float32r
BF16 = mybir.dt.bfloat16
I32 = mybir.dt.int32
ALU = mybir.AluOpType
ACT = mybir.ActivationFunctionType
AX = mybir.AxisListType

B, T, C = 128, 128, 64
HEADS, DH = 4, 64
E, H = 8, 128
GB = 4
NG = B // GB
GT = GB * T
VROWS = T + 1
ROW = 3 * C // 2 + C
SCALE = DH ** -0.5
EPS_LN = 1e-5
EPS_NRM = 1e-12
BIG = 3.0e38


def live(unit, count=NG):
    return not isinstance(unit, int) or 0 <= unit < count


def ge(eng, sem, value):
    if not isinstance(value, int) or value > 0:
        eng.wait_ge(sem, value)


def build_program(nc, x, emb_ext, w_in_t, b_oah, w_qkv, w_out_t, b_out, gamma, beta, w_r, b_r,
                  w1, b1_t, w2, b2, out):
    with ExitStack() as ctx:
        def sb(name, shape, dt=F32):
            return ctx.enter_context(nc.sbuf_tensor(name, shape, dt))

        def ps(name):
            return ctx.enter_context(nc.psum_tensor(name, [128, 512], F32))

        def sem(name):
            return ctx.enter_context(nc.semaphore(name))

        def ring(name, shape, dt=F32, n=2):
            return [sb(f"{name}{i}", shape, dt) for i in range(n)]

        ident = sb("ident", [128, 128])
        causal = sb("causal", [T, T], BF16)
        ones_col = sb("ones_col", [128, 1])
        ones_bf = sb("ones_bf", [128, 1], BF16)
        minus_half = sb("minus_half", [128, GB])
        x_int = sb("x_int", [B, T], I32)
        x_flt = sb("x_flt", [B, T])
        key = sb("key", [T, B])
        maskT = sb("maskT", [T, B])
        start_f = sb("start_f", [1, B])
        start_i = sb("start_i", [1, B], I32)
        emb_f = sb("emb_f", [128, 2, C])
        emb_rest = sb("emb_rest", [128, 2, C])
        emb_tab = sb("emb_tab", [128, 2, ROW])
        emb0 = sb("emb0", [1, C])
        emb0_sq = sb("emb0_sq", [1, C])
        nrm0 = sb("nrm0", [C, B])
        w_in_sb = sb("w_in_sb", [C, C])
        b_oah_bc = sb("b_oah_bc", [128, C])
        b_out_bc = sb("b_out_bc", [128, C])
        qkv = sb("qkv", [DH, 3 * HEADS, 2, C])
        wo = sb("wo", [DH, HEADS, C])
        m_hi = sb("m_hi", [128, HEADS * C], F32R)
        m_lo = sb("m_lo", [128, HEADS * C], F32R)
        n_hi = sb("n_hi", [128, HEADS * C], F32R)
        n_lo = sb("n_lo", [128, HEADS * C], F32R)
        w1_f = sb("w1_f", [128, E, H])
        w1_hi = sb("w1_hi", [128, E, H], F32R)
        w1_lo = sb("w1_lo", [128, E, H], F32R)
        b1_sb = sb("b1_sb", [H, E])
        w2_sb = sb("w2_sb", [H, E, C])
        b2_diag = sb("b2_diag", [GB * E, GB * C])
        wr_f = sb("wr_f", [128, E])
        wr_split = sb("wr_split", [128, 2, E], F32R)
        br_bc = sb("br_bc", [128, E])
        gamma2 = sb("gamma2", [128, 1])
        beta2 = sb("beta2", [128, 1])
        descend = sb("descend", [128, GB, E])

        resid = sb("resid", [T, B, C])

        ids = ring("ids", [128, GT], I32)
        pe_rows = ring("pe_rows", [T, GB, ROW])
        rel = ring("rel", [T, GB, T], BF16)
        n2 = ring("n2", [C, GB])
        n2g = ring("n2g", [C, GB])
        rn = ring("rn", [C, GB])
        p1s = ring("p1s", [C, GT])
        cnt = ring("cnt", [T, GB])
        rcnt = ring("rcnt", [T, GB])
        h0 = ring("h0", [T, GB, C])
        hcur = ring("hcur", [T, GB, C])
        hsum = ring("hsum", [T, GB])
        nmean = ring("nmean", [T, GB])
        xc = ring("xc", [T, GB, C])
        sq = ring("sq", [T, GB, C])
        vsum = ring("vsum", [T, GB])
        var = ring("var", [T, GB])
        rstd = ring("rstd", [T, GB])
        xn = ring("xn", [T, GB, 2, C])
        xdiag = ring("xdiag", [128, GB, 2, T])
        xs = ring("xs", [128, GT], F32R)
        z = [ring(f"z{p}", [128, GT]) for p in range(2)]
        u = ring("u", [T, GB, HEADS, C + 1])
        nmax = ring("nmax", [T, HEADS])
        prob = ring("prob", [T, HEADS, T])
        probT = ring("probT", [T, HEADS, T])
        rden = ring("rden", [T, HEADS])
        onorm = ring("onorm", [T, 2, HEADS, C])
        heads2 = ring("heads2", [T, 2, 2, C])
        attn = ring("attn", [T, 2, C])

        xT = ring("xT", [128, GT])
        xs2 = ring("xs2", [128, GT], F32R)
        lg_part = sb("lg_part", [T, GB, E])
        lg = ring("lg", [T, GB, E])
        top = ring("top", [T, GB])
        top2 = ring("top2", [T, GB])
        eq = ring("eq", [T, GB, E])
        rank = ring("rank", [T, GB, E])
        best = ring("best", [T, GB])
        hot1 = ring("hot1", [T, GB, E])
        hot2 = ring("hot2", [T, GB, E])
        rest = ring("rest", [T, GB, E])
        gap = ring("gap", [T, GB])
        th = ring("th", [T, GB])
        half = sb("half", [T, GB])
        whalf = ring("whalf", [T, GB])
        wfirst = ring("wfirst", [T, GB])
        hdif = ring("hdif", [T, GB, E])
        hmul = ring("hmul", [T, GB, E])
        wfull = ring("wfull", [T, GB, E])
        wT = ring("wT", [GB * E, T])
        hT = ring("hT", [H, E, GT])
        base = ring("base", [T, GB, C])
        prod = ring("prod", [T, E, C])
        moe = ring("moe", [T, GB, C])
        yout = ring("yout", [T, GB, C])

        table = nc.dram_tensor("table", (256, ROW), F32, kind="Internal").ap()

        S = [ps("psS0"), ps("psS1")]
        PT = [ps("psT0"), ps("psT1")]
        O = [ps("psO0"), ps("psO1")]
        M = [ps("psM0"), ps("psM1")]

        s_ld_x, s_ld_emb, s_ld_att, s_ld_ffn = (sem(n) for n in ("ld_x", "ld_emb", "ld_att", "ld_ffn"))
        s_const, s_zero, s_one = sem("const"), sem("zero"), sem("one")
        s_causal = sem("causal_done")
        s_xflt, s_xT, s_keyT, s_len, s_start, s_startf = (sem(n) for n in ("xflt", "xTd", "keyT", "len", "start", "startf"))
        s_emb, s_table, s_e0, s_n0, s_nrm0 = (sem(n) for n in ("emb", "tabled", "e0", "n0", "nrm0d"))
        s_fold, s_split, s_w1 = sem("fold"), sem("split"), sem("w1split")
        s_b2z = sem("b2z")
        s_ids = [sem("ids_a"), sem("ids_b")]
        s_rows = [sem("rows_a"), sem("rows_b")]
        (s_rel, pe_n2, s_n2, s_n2g, s_rn, pe_p1, s_p1s, pe_o1, s_cnt, s_rcnt, s_h0, s_h, s_hsum, s_nmean,
         s_xc, s_sq, s_vsum, s_var, s_rstd, s_xn, s_base_h) = (
            sem(f"a_{n}") for n in ("rel", "pe_n2", "n2", "n2g", "rn", "pe_p1", "p1s", "pe_o1", "cnt", "rcnt", "h0",
                                    "h", "hsum", "nmean", "xc", "sq", "vsum", "var", "rstd", "xn", "base_h"))
        (pe_d, s_xdiag, s_xhi, s_xs, pe_z, s_z, pe_u01, pe_u23, s_u01, s_u23) = (
            sem(f"a_{n}") for n in ("pe_d", "xdiag", "xhi", "xs", "pe_z", "z", "pe_u01", "pe_u23", "u01", "u23"))
        (pe_dots, s_nmax, s_exp, pe_t, s_pt, pe_v, s_rden, s_on, s_attn, s_h1) = (
            sem(f"a_{n}") for n in ("pe_dots", "nmax", "exp", "pe_t", "pt", "pe_v", "rden", "on", "attn", "h1"))
        (b_hsum, b_nmean, b_xc, b_sq, b_vsum, b_var, b_rstd, b_xn, bpe_d, b_xT, b_xhi, b_xs) = (
            sem(f"b_{n}") for n in ("hsum", "nmean", "xc", "sq", "vsum", "var", "rstd", "xn", "pe_d", "xT", "xhi", "xs"))
        (bpe_lg, b_lg, b_top, b_eq, b_rank, b_best, b_hot1, b_rest, b_top2, b_eq2, b_rank2, b_best2, b_hot2,
         b_gap, b_th, b_wfirst, b_hdif, b_hmul, b_w, bpe_wT, b_wT, bpe_yb, b_base) = (
            sem(f"b_{n}") for n in ("pe_lg", "lg", "top", "eq", "rank", "best", "hot1", "rest", "top2", "eq2", "rank2",
                                    "best2", "hot2", "gap", "th", "wfirst", "hdif", "hmul", "w", "pe_wT", "wT",
                                    "pe_yb", "base"))
        (bpe_l1, b_gelu, bpe_y, b_prod, b_moe, b_final) = (
            sem(f"b_{n}") for n in ("pe_l1", "gelu", "pe_y", "prod", "moe", "out"))
        s_heads2 = sem("a_heads2")
        b_whalf, b_lg_part = sem("b_whalf"), sem("b_lg_part")
        s_store = [sem("store_a"), sem("store_b")]

        block = ctx.enter_context(nc.Block())

        ids_flat = x.rearrange("b t -> (b t)")
        LOOP_A = (4, 30)
        STEPS_A = NG + 2
        LOOP_B = (4, 32)
        FFN_LOADED = 16 * (11 + GB)
        STEPS_B = NG + 3

        def sweep(eng, step, loop, steps):
            for k in range(loop[0]):
                step(k, k % 2)
            with eng.Fori(loop[0] // 2, loop[1] // 2) as i:
                step(2 * i, 0)
                step(2 * i + 1, 1)
            for k in range(loop[1], steps):
                step(k, k % 2)

        @block.sync
        def _(sp):
            sp.dma_start(x_int[:], x).then_inc(s_ld_x, 16)
            sp.dma_start(emb_f[:], emb_ext.rearrange("(c p) n -> p c n", p=128)).then_inc(s_ld_emb, 16)
            sp.dma_start(emb0[:], emb_ext[T:T + 1, :]).then_inc(s_ld_emb, 16)
            for d in range(2):
                sp.dma_start(qkv[:, :, d, :], w_qkv.rearrange("(c e) d -> e c d", e=DH)).then_inc(s_ld_att, 16)
            sp.dma_start(wo[:], w_out_t.rearrange("(h e) o -> e h o", e=DH)).then_inc(s_ld_att, 16)
            sp.dma_start(w_in_sb[:], w_in_t).then_inc(s_ld_att, 16)
            sp.dma_start(b_oah_bc[:], b_oah.partition_broadcast(128)).then_inc(s_ld_att, 16)
            sp.dma_start(b_out_bc[:], b_out.partition_broadcast(128)).then_inc(s_ld_att, 16)
            sp.wait_ge(s_emb, 1)
            sp.dma_start(table.rearrange("(c p) n -> p c n", p=128), emb_tab[:]).then_inc(s_table, 16)
            sp.wait_ge(s_table, 16)
            sp.wait_ge(s_start, 1)

            def step(k, par):
                ge(sp, s_rel, k - 1)
                sp.dma_start(ids[par][:], ids_flat[bass.ds(k * GT, GT)].partition_broadcast(128)) \
                  .then_inc(s_ids[par], 16)
                ge(sp, pe_p1, k - 1)
                for b in range(GB):
                    first = sp.value_load(start_i[0:1, bass.ds(k * GB + b, 1)], min_val=0, max_val=T)
                    sp.dma_start(pe_rows[par][:, b, :], table[bass.ds(first, T), :]).then_inc(s_rows[par], 16)

            sweep(sp, step, (2, NG), NG)

            def store(k, par):
                ge(sp, b_final, k + 1)
                sp.dma_start(out[bass.ds(k * GB, GB)].rearrange("b t c -> t b c"), yout[par][:]) \
                  .then_inc(s_store[par], 16)

            sweep(sp, store, (2, NG), NG)
            for par in range(2):
                sp.wait_ge(s_store[par], 16 * NG // 2)

        @block.gpsimd
        def _(pool):
            pool.memset(ident[:], 0.0).then_inc(s_zero, 1)
            pool.memset(causal[:], 1.0).then_inc(s_one, 1)
            pool.wait_ge(s_zero, 1)
            pool.affine_select(out=ident[:], in_=ident[:], compare_op=ALU.not_equal, fill=1.0, base=0,
                               pattern=[[-1, 128]], channel_multiplier=1).then_inc(s_const, 1)
            pool.wait_ge(s_one, 1)
            pool.affine_select(out=causal[:], in_=causal[:], compare_op=ALU.is_ge, fill=0.0, base=0,
                               pattern=[[-1, T]], channel_multiplier=1).then_inc(s_causal, 1)
            pool.memset(b2_diag[:], 0.0).then_inc(s_b2z, 1)
            pool.dma_start(w1_f[0:C], w1.rearrange("e d h -> d e h")).then_inc(s_ld_ffn, 16)
            pool.dma_start(w1_f[C:128], w1.rearrange("e d h -> d e h")).then_inc(s_ld_ffn, 16)
            pool.dma_start(b1_sb[:], b1_t).then_inc(s_ld_ffn, 16)
            pool.dma_start(w2_sb[:], w2.rearrange("e h c -> h e c")).then_inc(s_ld_ffn, 16)
            pool.dma_start(br_bc[:], b_r.partition_broadcast(128)).then_inc(s_ld_ffn, 16)
            for d in range(2):
                pool.dma_start(wr_f[d * C:d * C + C], w_r).then_inc(s_ld_ffn, 16)
                pool.dma_start(gamma2[d * C:d * C + C], gamma.unsqueeze(1)).then_inc(s_ld_ffn, 16)
                pool.dma_start(beta2[d * C:d * C + C], beta.unsqueeze(1)).then_inc(s_ld_ffn, 16)
            pool.wait_ge(s_b2z, 1)
            for b in range(GB):
                pool.dma_start(b2_diag[b * E:b * E + E, b * C:b * C + C], b2).then_inc(s_ld_ffn, 16)

            pool.wait_ge(s_split, 1)
            pool.wait_ge(s_ld_att, 96)

            def add_pair(m_attn, col, par):
                ge(pool, s_on, 2 * m_attn + 2)
                ge(pool, s_attn, m_attn - 1)
                pool.tensor_tensor(heads2[par][:], onorm[par][:, :, 0:2, :], onorm[par][:, :, 2:4, :], ALU.add) \
                    .then_inc(s_heads2, 1)
                pool.wait_ge(s_heads2, m_attn + 1)
                ge(pool, s_h1, m_attn - 1)
                pool.tensor_tensor(attn[par][:], heads2[par][:, :, 0, :], heads2[par][:, :, 1, :], ALU.add) \
                    .then_inc(s_attn, 1)
                pool.wait_ge(s_attn, m_attn + 1)
                dst = resid[:, bass.ds(col, 2), :]
                pool.tensor_tensor(dst, dst, attn[par][:], ALU.add).then_inc(s_h1, 1)

            def step(k, par):
                a = k - 2
                if live(k):
                    ge(pool, s_p1s, k - 1)
                    pool.wait_ge(s_n2g, k + 1)
                    pool.tensor_tensor(rn[par][:], n2g[par][:], minus_half[0:C, :], ALU.pow).then_inc(s_rn, 1)
                if live(a - 1):
                    ge(pool, s_base_h, a)
                    add_pair(2 * (a - 1), (a - 1) * GB, 0)
                if live(k):
                    pool.wait_ge(s_h0, k + 1)
                    ge(pool, s_hsum, k - 1)
                    ge(pool, s_base_h, k - 1)
                    pool.tensor_tensor(hcur[par][:], h0[par][:], b_oah_bc[:].unsqueeze(1).broadcast_to([T, GB, C]),
                                       ALU.add).then_inc(s_h, 1)
                    pool.wait_ge(s_h, k + 1)
                    pool.tensor_tensor(resid[:, bass.ds(k * GB, GB), :], hcur[par][:],
                                       b_out_bc[:].unsqueeze(1).broadcast_to([T, GB, C]), ALU.add).then_inc(s_base_h, 1)
                    pool.wait_ge(s_nmean, k + 1)
                    ge(pool, s_xn, k - 1)
                    pool.tensor_tensor(xc[par][:], hcur[par][:], nmean[par][:].unsqueeze(2).broadcast_to([T, GB, C]),
                                       ALU.add).then_inc(s_xc, 1)
                    ge(pool, s_vsum, k - 1)
                    pool.wait_ge(s_xc, k + 1)
                    pool.tensor_tensor(sq[par][:], xc[par][:], xc[par][:], ALU.mult).then_inc(s_sq, 1)
                if live(a - 1):
                    add_pair(2 * (a - 1) + 1, (a - 1) * GB + 2, 1)
                if live(k):
                    pool.wait_ge(s_var, k + 1)
                    pool.tensor_tensor(rstd[par][:], var[par][:], minus_half[:], ALU.pow).then_inc(s_rstd, 1)

            sweep(pool, step, LOOP_A, STEPS_A + 1)

            def expert_step(k, par):
                opp = 1 - par
                if live(k - 2):
                    g = k - 2
                    pool.wait_ge(b_th, g + 1)
                    pool.tensor_tensor(whalf[par][:], th[par][:], half[:], ALU.mult).then_inc(b_whalf, 1)
                    pool.wait_ge(b_whalf, g + 1)
                    ge(pool, b_hmul, g - 1)
                    pool.tensor_tensor(wfirst[par][:], whalf[par][:], half[:], ALU.add).then_inc(b_wfirst, 1)
                    pool.wait_ge(b_hot2, g + 1)
                    pool.tensor_tensor(hdif[par][:], hot1[par][:], hot2[par][:], ALU.subtract).then_inc(b_hdif, 1)
                    pool.wait_ge(b_hdif, g + 1)
                    pool.wait_ge(b_wfirst, g + 1)
                    pool.tensor_tensor(hmul[par][:], hdif[par][:],
                                       wfirst[par][:].unsqueeze(2).broadcast_to([T, GB, E]), ALU.mult).then_inc(b_hmul, 1)
                    ge(pool, b_prod, 4 * (g - 1))
                    ge(pool, bpe_wT, g - 1)
                    pool.wait_ge(b_hmul, g + 1)
                    pool.tensor_tensor(wfull[par][:], hmul[par][:], hot2[par][:], ALU.add).then_inc(b_w, 1)
                if live(k):
                    pool.wait_ge(b_nmean, k + 1)
                    ge(pool, b_xn, k - 1)
                    pool.tensor_tensor(xc[par][:], resid[:, bass.ds(k * GB, GB), :],
                                       nmean[par][:].unsqueeze(2).broadcast_to([T, GB, C]), ALU.add).then_inc(b_xc, 1)
                    ge(pool, b_vsum, k - 1)
                    pool.wait_ge(b_xc, k + 1)
                    pool.tensor_tensor(sq[par][:], xc[par][:], xc[par][:], ALU.mult).then_inc(b_sq, 1)
                if live(k):
                    pool.wait_ge(b_var, k + 1)
                    pool.tensor_tensor(rstd[par][:], var[par][:], minus_half[:], ALU.pow).then_inc(b_rstd, 1)
                if live(k - 3):
                    g = k - 3
                    pool.wait_ge(b_moe, 4 * (g + 1))
                    pool.wait_ge(b_base, g + 1)
                    ge(pool, s_store[opp], 8 * (g - opp))
                    pool.tensor_tensor(yout[opp][:], moe[opp][:], base[opp][:], ALU.add).then_inc(b_final, 1)

            pool.wait_ge(s_xn, NG)
            sweep(pool, expert_step, LOOP_B, STEPS_B)

        @block.tensor
        def _(pe):
            pe.wait_ge(s_const, 1)
            pe.wait_ge(s_xflt, 1)
            pe.transpose(M[0][:, 0:B], x_flt[:], ident[:]).then_inc(s_xT, 1)
            pe.wait_ge(s_keyT, 2)
            pe.matmul(M[1][0:1, 0:B], ones_col[:], maskT[:], start=True, stop=True).then_inc(s_len, 1)
            pe.wait_ge(s_startf, 1)
            pe.wait_ge(s_e0, 1)
            pe.matmul(O[0][0:C, 0:B], emb0_sq[:], start_f[:], start=True, stop=True).then_inc(s_n0, 1)
            pe.wait_ge(s_ld_att, 96)
            for h in range(HEADS):
                pe.matmul(S[0][:, h * C:h * C + C], qkv[:, h, :, :], qkv[:, HEADS + h, 0, :], start=True, stop=True)
            for h in range(HEADS):
                last = pe.matmul(S[1][:, h * C:h * C + C], qkv[:, 2 * HEADS + h, :, :], wo[:, h, :],
                                 start=True, stop=True)
            last.then_inc(s_fold, 1)
            pe.wait_ge(s_split, 1)
            pe.wait_ge(s_nrm0, 1)
            pe.wait_ge(s_keyT, 3)

            def dots(s, b, par, a):
                q = b % 2
                if b == 0:
                    ge(pe, s_z, a + 1)
                ge(pe, s_exp, s - 1)
                for p in range(2):
                    last = pe.matmul(S[q][:, 2 * p * T:2 * p * T + 2 * T], z[p][par][:, b * T:b * T + T],
                                     xdiag[par][:, b, :, :], start=True, stop=True)
                last.then_inc(pe_dots, 1)

            def turn(s, q):
                ge(pe, s_exp, s + 1)
                ge(pe, s_pt, s - 1)
                for h in range(HEADS):
                    last = pe.transpose(PT[q][:, h * T:h * T + T], prob[q][:, h, :], ident[:])
                last.then_inc(pe_t, 1)

            def weigh(s, b, par, g):
                q = b % 2
                if b == 0:
                    ge(pe, s_u01, g + 1)
                    ge(pe, s_u23, g + 1)
                ge(pe, s_pt, s + 1)
                ge(pe, s_on, s - 1)
                for h in range(HEADS):
                    last = pe.matmul(O[q][:, h * (C + 1):(h + 1) * (C + 1)], probT[q][:, h, :], u[par][:, b, h, :],
                                     start=True, stop=True)
                last.then_inc(pe_v, 1)

            def step(k, par):
                a, opp = k - 2, 1 - par
                if live(a):
                    dots(4 * a, 0, par, a)
                if live(k):
                    rows = pe_rows[par][:].bitcast(BF16)
                    pe.wait_ge(s_rows[par], 32 * (k - par) + 64)
                    ge(pe, s_u01, k - 1)
                    for b in range(GB):
                        last = pe.matmul(M[1][0:C, b:b + 1], pe_rows[par][:, b, 3 * C // 2:ROW],
                                         maskT[:, bass.ds(k * GB + b, 1)], start=True, stop=True)
                    last.then_inc(pe_n2, 1)
                    pe.wait_ge(s_rel, k + 1)
                    ge(pe, s_u23, k - 1)
                    ge(pe, s_h0, k)
                    for b in range(GB):
                        for part in range(3):
                            last = pe.matmul(M[0][0:C, b * T:b * T + T], rows[:, b, part * C:part * C + C],
                                             rel[par][:, b, :], start=(part == 0), stop=(part == 2))
                    last.then_inc(pe_p1, 1)
                if live(a - 1):
                    turn(4 * a - 1, 1)
                    weigh(4 * a - 2, 2, opp, a - 1)
                if live(k - 1):
                    pe.wait_ge(s_xn, k)
                    ge(pe, s_n2, k + 1 if live(k) else 0)
                    for b in range(GB):
                        last = pe.transpose(M[1][:, b * T:b * T + T], xn[opp][:, b, :, :], ident[:])
                    last.then_inc(pe_d, 1)
                if live(a):
                    dots(4 * a + 1, 1, par, a)
                if live(a):
                    turn(4 * a, 0)
                if live(k):
                    pe.wait_ge(s_p1s, k + 1)
                    for b in range(GB):
                        pe.matmul(M[0][:, GB * C + b:GB * C + b + 1], rel[par][:, b, :], ones_bf[:], start=True, stop=True)
                    for b in range(GB):
                        last = pe.matmul(M[0][:, b * C:b * C + C], p1s[par][:, b * T:b * T + T], w_in_sb[:],
                                         start=True, stop=True)
                    last.then_inc(pe_o1, 1)
                if live(a - 1):
                    weigh(4 * a - 1, 3, opp, a - 1)
                if live(a):
                    dots(4 * a + 2, 2, par, a)
                    turn(4 * a + 1, 1)
                if live(k - 1):
                    pe.wait_ge(s_xs, k)
                    pe.wait_ge(s_xdiag, k)
                    ge(pe, s_h0, k + 1 if live(k) else 0)
                    for p in range(2):
                        bank = M[1 - p]
                        pe.matmul(bank[:], m_hi[:, p * 2 * C:(p + 1) * 2 * C], xs[opp][:], start=True, stop=False)
                        last = pe.matmul(bank[:], m_lo[:, p * 2 * C:(p + 1) * 2 * C], xs[opp][:], start=False, stop=True)
                    last.then_inc(pe_z, 1)
                if live(a):
                    weigh(4 * a, 0, par, a)
                if live(a):
                    dots(4 * a + 3, 3, par, a)
                if live(k - 1):
                    pe.wait_ge(s_z, k)
                    for half, done in ((0, pe_u01), (1, pe_u23)):
                        bank = M[1 - half]
                        for b in range(2):
                            tok = (2 * half + b) * T
                            dst = bank[:, b * HEADS * C:(b + 1) * HEADS * C]
                            pe.matmul(dst, xs[opp][:, tok:tok + T], n_hi[:], start=True, stop=False)
                            last = pe.matmul(dst, xs[opp][:, tok:tok + T], n_lo[:], start=False, stop=True)
                        last.then_inc(done, 1)
                if live(a):
                    turn(4 * a + 2, 0)
                    weigh(4 * a + 1, 1, par, a)

            sweep(pe, step, LOOP_A, STEPS_A + 1)

            pe.wait_ge(s_exp, B)
            pe.wait_ge(s_pt, B)
            pe.wait_ge(s_on, B)
            pe.wait_ge(s_u01, NG)
            pe.wait_ge(s_u23, NG)
            pe.wait_ge(s_ld_ffn, FFN_LOADED)
            pe.wait_ge(s_w1, 2)
            L, Y, Dp, Lg, Wb = S, O, PT[0], PT[1], M[0]

            def expert_step(k, par):
                opp = 1 - par
                for e in range(E):
                    if live(k - 2):
                        g, n = k - 2, 8 * (k - 2) + e
                        if e == 0:
                            pe.wait_ge(b_xs, g + 1)
                        ge(pe, b_gelu, n - 1)
                        pe.matmul(L[e % 2][:], w1_hi[:, e, :], xs2[par][:], start=True, stop=False)
                        pe.matmul(L[e % 2][:], w1_lo[:, e, :], xs2[par][:], start=False, stop=True).then_inc(bpe_l1, 1)
                    if e == 1 and live(k - 1):
                        pe.wait_ge(b_xn, k)
                        ge(pe, b_xT, k - 1)
                        for b in range(GB):
                            last = pe.transpose(Dp[:, b * T:b * T + T], xn[opp][:, b, :, :], ident[:])
                        last.then_inc(bpe_d, 1)
                    if e == 5 and live(k - 1):
                        pe.wait_ge(b_xs, k)
                        ge(pe, b_lg, k - 1)
                        for b in range(GB):
                            last = pe.matmul(Lg[:, b * 2 * E:(b + 1) * 2 * E], xs2[opp][:, b * T:b * T + T], wr_split[:],
                                             start=True, stop=True)
                        last.then_inc(bpe_lg, 1)
                    if e == 4 and live(k - 2):
                        pe.wait_ge(b_w, k - 1)
                        ge(pe, b_base, k - 2)
                        pe.transpose(Wb[0:GB * E, 256:256 + T], wfull[par][:], ident[:]).then_inc(bpe_wT, 1)
                    if e == 7 and live(k - 2):
                        pe.wait_ge(b_wT, k - 1)
                        pe.matmul(Wb[:, 0:GB * C], wT[par][:], b2_diag[:], start=True, stop=True).then_inc(bpe_yb, 1)
                    if live(k - 3):
                        g, b = k - 3, e // 2
                        if e == 0:
                            pe.wait_ge(b_gelu, 8 * (g + 1))
                        if e % 2 == 0:
                            ge(pe, b_prod, 4 * g + b - 1)
                        for i in range(4 * (e % 2), 4 * (e % 2) + 4):
                            last = pe.matmul(Y[b % 2][:, i * C:i * C + C], hT[opp][:, i, b * T:b * T + T], w2_sb[:, i, :],
                                             start=True, stop=True)
                        if e % 2:
                            last.then_inc(bpe_y, 1)

            sweep(pe, expert_step, LOOP_B, STEPS_B)

        @block.scalar
        def _(act):
            def exps(s, q):
                ge(act, s_nmax, s + 1)
                ge(act, pe_t, s - 1)
                for h in range(HEADS):
                    last = act.activation(prob[q][:, h, :], S[q][:, h * T:h * T + T], ACT.Exp, bias=nmax[q][:, h:h + 1])
                last.then_inc(s_exp, 1)

            def take_turned(s, q):
                ge(act, pe_t, s + 1)
                ge(act, pe_v, s - 1)
                act.copy(probT[q][:], PT[q][:].rearrange("p (h i) -> p h i", h=HEADS)).then_inc(s_pt, 1)

            act.wait_ge(s_split, 1)

            def step(k, par):
                a, opp = k - 2, 1 - par
                if live(a):
                    exps(4 * a, 0)
                if live(a - 1):
                    take_turned(4 * a - 1, 1)
                if live(k - 1):
                    act.wait_ge(pe_d, k)
                    ge(act, pe_dots, 4 * (k - 2))
                    ge(act, s_xs, k - 2)
                    src = M[1][:].rearrange("p (b t) -> p b t", b=GB)
                    act.copy(xdiag[opp][0:C, :, 0, :], src[0:C])
                    act.copy(xdiag[opp][C:128, :, 1, :], src[C:128]).then_inc(s_xdiag, 1)
                if live(a):
                    exps(4 * a + 1, 1)
                if live(a):
                    take_turned(4 * a, 0)
                if live(a):
                    exps(4 * a + 2, 0)
                if live(k - 1):
                    act.wait_ge(pe_z, k)
                    ge(act, pe_dots, 4 * (k - 2))
                    act.copy(z[0][opp][:], M[1][:])
                    act.copy(z[1][opp][:], M[0][:]).then_inc(s_z, 1)
                if live(a):
                    take_turned(4 * a + 1, 1)
                if live(a):
                    exps(4 * a + 3, 1)
                if live(k - 1):
                    act.wait_ge(pe_u01, k)
                    ge(act, pe_v, 4 * (k - 2))
                    act.copy(u[opp][:, 0:2, :, 0:C], M[1][:].rearrange("p (b h c) -> p b h c", b=2, h=HEADS)) \
                       .then_inc(s_u01, 1)
                    act.wait_ge(pe_u23, k)
                    act.copy(u[opp][:, 2:4, :, 0:C], M[0][:].rearrange("p (b h c) -> p b h c", b=2, h=HEADS)) \
                       .then_inc(s_u23, 1)
                if live(a):
                    take_turned(4 * a + 2, 0)

            sweep(act, step, LOOP_A, STEPS_A + 1)

            act.wait_ge(s_ld_ffn, FFN_LOADED)

            def expert_step(k, par):
                opp = 1 - par
                for e in range(E):
                    if live(k - 2):
                        g, n = k - 2, 8 * (k - 2) + e
                        act.wait_ge(bpe_l1, n + 1)
                        if e % 2 == 0:
                            ge(act, bpe_y, 4 * (g - 1))
                        act.activation(hT[par][:, e, :], L[e % 2][:], ACT.Gelu, bias=b1_sb[:, e:e + 1]).then_inc(b_gelu, 1)
                    if e == 0 and live(k - 2):
                        g = k - 2
                        act.wait_ge(b_gap, g + 1)
                        ge(act, b_wfirst, g - 1)
                        act.activation(th[par][:], gap[par][:], ACT.Tanh, scale=0.5).then_inc(b_th, 1)
                    if e == 2 and live(k - 1):
                        act.wait_ge(bpe_d, k)
                        ge(act, b_xs, k - 2)
                        act.activation(xT[opp][:], Dp[:], ACT.Identity, scale=gamma2[:], bias=beta2[:]).then_inc(b_xT, 1)
                    if e == 5 and live(k - 2):
                        act.wait_ge(bpe_wT, k - 1)
                        ge(act, bpe_yb, k - 3)
                        act.copy(wT[par][:], Wb[0:GB * E, 256:256 + T]).then_inc(b_wT, 1)

            L, Dp, Wb = S, PT[0], M[0]
            sweep(act, expert_step, LOOP_B, STEPS_B)

        @block.vector
        def _(dve):
            dve.memset(ones_col[:], 1.0)
            dve.memset(ones_bf[:], 1.0)
            dve.memset(minus_half[:], -0.5)
            dve.memset(half[:], 0.5)
            dve.memset(emb_tab[:], 0.0)
            for r in range(2):
                dve.memset(xdiag[r][:], 0.0)
                dve.memset(u[r][:, :, :, C:C + 1], 1.0)
            for w in (m_lo, n_lo):
                dve.memset(w[C:128].bitcast(F32), 0.0)
            dve.memset(w1_lo[C:128].bitcast(F32), 0.0)
            dve.memset(wr_split[C:128, 1].bitcast(F32), 0.0)
            for e in range(E):
                dve.memset(descend[:, :, e:e + 1], float(E - e))
            dve.wait_ge(s_ld_x, 16)
            dve.tensor_copy(x_flt[:], x_int[:]).then_inc(s_xflt, 1)
            dve.wait_ge(s_xT, 1)
            dve.tensor_scalar(maskT[:], M[0][:, 0:B], 0.0, None, ALU.not_equal).then_inc(s_keyT, 1)
            dve.tensor_scalar(key[:], M[0][:, 0:B], 0.0, -0.5, ALU.is_equal, ALU.mult).then_inc(s_keyT, 1)
            dve.wait_ge(s_keyT, 2)
            dve.tensor_tensor(key[:], key[:], M[0][:, 0:B], ALU.add).then_inc(s_keyT, 1)
            dve.wait_ge(s_len, 1)
            dve.tensor_scalar(start_f[:], M[1][0:1, 0:B], -1.0, float(T), ALU.mult, ALU.add).then_inc(s_startf, 1)
            dve.wait_ge(s_startf, 1)
            dve.tensor_copy(start_i[:], start_f[:]).then_inc(s_start, 1)
            chain = s_emb_chain = sem("emb_chain")
            dve.wait_ge(s_ld_emb, 32)
            dve.tensor_tensor(emb0_sq[:], emb0[:], emb0[:], ALU.mult).then_inc(s_e0, 1)
            parts = emb_tab[:].bitcast(BF16)
            dve.tensor_copy(parts[:, :, 0:C], emb_f[:]).then_inc(chain, 1)
            dve.tensor_tensor(emb_tab[:, :, 3 * C // 2:ROW], emb_f[:], emb_f[:], ALU.mult)
            dve.wait_ge(chain, 1)
            dve.tensor_tensor(emb_rest[:], emb_f[:], parts[:, :, 0:C], ALU.subtract).then_inc(chain, 1)
            dve.wait_ge(chain, 2)
            dve.tensor_copy(parts[:, :, C:2 * C], emb_rest[:]).then_inc(chain, 1)
            dve.wait_ge(chain, 3)
            dve.tensor_tensor(emb_rest[:], emb_rest[:], parts[:, :, C:2 * C], ALU.subtract).then_inc(chain, 1)
            dve.wait_ge(chain, 4)
            dve.tensor_copy(parts[:, :, 2 * C:3 * C], emb_rest[:]).then_inc(s_emb, 1)
            dve.wait_ge(s_n0, 1)
            dve.tensor_copy(nrm0[:], O[0][0:C, 0:B]).then_inc(s_nrm0, 1)
            dve.wait_ge(s_fold, 1)
            dve.tensor_scalar(m_hi[:], S[0][:, 0:HEADS * C], SCALE, None, ALU.mult)
            dve.tensor_copy(n_hi[:], S[1][:, 0:HEADS * C]).then_inc(chain, 1)
            dve.wait_ge(chain, 5)
            dve.scalar_tensor_tensor(m_lo[0:C], S[0][0:C, 0:HEADS * C], SCALE, m_hi[0:C].bitcast(F32), ALU.mult, ALU.subtract)
            dve.tensor_tensor(n_lo[0:C], S[1][0:C, 0:HEADS * C], n_hi[0:C].bitcast(F32), ALU.subtract).then_inc(s_split, 1)

            def relation(k, par):
                dve.wait_ge(s_ids[par], 8 * (k - par) + 16)
                ge(dve, pe_o1, k - 1)
                for b in range(GB):
                    last = dve.scalar_tensor_tensor(rel[par][:, b, :], ids[par][:, b * T:b * T + T],
                                                    key[:, bass.ds(k * GB + b, 1)], causal[:], ALU.is_equal, ALU.mult)
                last.then_inc(s_rel, 1)

            def maxima(s, q):
                ge(dve, pe_dots, s + 1)
                ge(dve, s_exp, s - 1)
                dve.tensor_reduce(nmax[q][:], S[q][:].rearrange("p (h j) -> p h j", h=HEADS), AX.X, ALU.max,
                                  negate=True).then_inc(s_nmax, 1)

            def combine(s, b, freed):
                q, m, half = b % 2, b // 2, b % 2
                ge(dve, pe_v, s + 1)
                src = O[q][:, 0:HEADS * (C + 1)].rearrange("p (h c) -> p h c", h=HEADS)
                ge(dve, s_on, s - 1)
                if half == 0:
                    ge(dve, s_heads2, freed)
                dve.reciprocal(rden[q][:], src[:, :, C]).then_inc(s_rden, 1)
                ge(dve, s_rden, s + 1)
                dve.tensor_tensor(onorm[m][:, half], src[:, :, 0:C], rden[q][:].unsqueeze(2).broadcast_to([T, HEADS, C]),
                                  ALU.mult).then_inc(s_on, 1)

            dve.wait_ge(s_causal, 1)
            dve.wait_ge(s_keyT, 3)
            relation(0, 0)

            def step(k, par):
                a, opp = k - 2, 1 - par
                if live(a):
                    maxima(4 * a, 0)
                if live(k):
                    dve.wait_ge(pe_n2, k + 1)
                    dve.tensor_tensor(n2[par][:], M[1][0:C, 0:GB], nrm0[:, bass.ds(k * GB, GB)], ALU.add).then_inc(s_n2, 1)
                    ge(dve, s_rn, k - 1)
                    dve.wait_ge(s_n2, k + 1)
                    dve.tensor_scalar(n2g[par][:], n2[par][:], EPS_NRM ** 2, None, ALU.max).then_inc(s_n2g, 1)
                if live(k + 1):
                    relation(k + 1, opp)
                if live(a - 1):
                    combine(4 * a - 2, 2, 2 * a - 2)
                if live(k):
                    dve.wait_ge(pe_p1, k + 1)
                    dve.wait_ge(s_rn, k + 1)
                    ge(dve, pe_o1, k - 1)
                    dve.tensor_tensor(p1s[par][:].rearrange("p (b t) -> p b t", b=GB),
                                      M[0][0:C, :].rearrange("p (b t) -> p b t", b=GB),
                                      rn[par][:].unsqueeze(2).broadcast_to([C, GB, T]), ALU.mult).then_inc(s_p1s, 1)
                if live(a):
                    maxima(4 * a + 1, 1)
                if live(k - 1):
                    dve.wait_ge(s_xdiag, k)
                    ge(dve, pe_u23, k - 2)
                    xs_v = xs[opp][:].rearrange("p (b t) -> p b t", b=GB)
                    dve.tensor_copy(xs_v[C:128], xdiag[opp][C:128, :, 1, :]).then_inc(s_xhi, 1)
                    dve.tensor_copy(xs_v[0:C], xdiag[opp][0:C, :, 0, :])
                    dve.wait_ge(s_xhi, k)
                    dve.tensor_tensor(xs_v[C:128], xdiag[opp][C:128, :, 1, :], xs_v[C:128].bitcast(F32),
                                      ALU.subtract).then_inc(s_xs, 1)
                if live(k):
                    dve.wait_ge(pe_o1, k + 1)
                    ge(dve, s_rcnt, k - 1)
                    dve.tensor_scalar(cnt[par][:], M[0][:, GB * C:GB * C + GB], 1.0, None, ALU.max).then_inc(s_cnt, 1)
                    dve.wait_ge(s_cnt, k + 1)
                    ge(dve, s_h0, k - 1)
                    dve.reciprocal(rcnt[par][:], cnt[par][:]).then_inc(s_rcnt, 1)
                    dve.wait_ge(s_rcnt, k + 1)
                    ge(dve, s_h, k - 1)
                    dve.tensor_tensor(h0[par][:], M[0][:, 0:GB * C].rearrange("p (b c) -> p b c", b=GB),
                                      rcnt[par][:].unsqueeze(2).broadcast_to([T, GB, C]), ALU.mult).then_inc(s_h0, 1)
                if live(a - 1):
                    combine(4 * a - 1, 3, 0)
                if live(a):
                    maxima(4 * a + 2, 0)
                if live(k):
                    dve.wait_ge(s_h, k + 1)
                    ge(dve, s_nmean, k - 1)
                    dve.tensor_reduce(hsum[par][:], hcur[par][:], AX.X, ALU.add).then_inc(s_hsum, 1)
                    dve.wait_ge(s_hsum, k + 1)
                    ge(dve, s_xc, k - 1)
                    dve.tensor_scalar(nmean[par][:], hsum[par][:], -1.0 / C, None, ALU.mult).then_inc(s_nmean, 1)
                if live(a):
                    combine(4 * a, 0, 2 * a - 1)
                if live(a):
                    maxima(4 * a + 3, 1)
                if live(k):
                    dve.wait_ge(s_sq, k + 1)
                    ge(dve, s_var, k - 1)
                    dve.tensor_reduce(vsum[par][:], sq[par][:], AX.X, ALU.add).then_inc(s_vsum, 1)
                    ge(dve, s_rstd, k - 1)
                    dve.wait_ge(s_vsum, k + 1)
                    dve.tensor_scalar(var[par][:], vsum[par][:], 1.0 / C, EPS_LN, ALU.mult, ALU.add).then_inc(s_var, 1)
                if live(a):
                    combine(4 * a + 1, 1, 0)
                if live(k):
                    dve.wait_ge(s_rstd, k + 1)
                    ge(dve, pe_d, k - 1)
                    dve.tensor_tensor(xn[par][:], xc[par][:].unsqueeze(2).broadcast_to([T, GB, 2, C]),
                                      rstd[par][:].unsqueeze(2).unsqueeze(3).broadcast_to([T, GB, 2, C]),
                                      ALU.mult).then_inc(s_xn, 1)

            sweep(dve, step, LOOP_A, STEPS_A + 1)

            dve.wait_ge(s_ld_ffn, FFN_LOADED)
            dve.tensor_copy(wr_split[:, 0], wr_f[:])
            dve.tensor_copy(w1_hi[:], w1_f[:]).then_inc(s_w1, 1)
            dve.wait_ge(s_w1, 1)
            dve.tensor_tensor(wr_split[0:C, 1], wr_f[0:C], wr_split[0:C, 0].bitcast(F32), ALU.subtract)
            dve.tensor_tensor(w1_lo[0:C], w1_f[0:C], w1_hi[0:C].bitcast(F32), ALU.subtract).then_inc(s_w1, 1)
            dve.wait_ge(s_rstd, NG)
            dve.wait_ge(pe_d, NG)
            L, Y, Dp, Lg, Wb = S, O, PT[0], PT[1], M[0]

            def bcast(t, n):
                return t[:].unsqueeze(2).broadcast_to([T, GB, n])

            def route(g, r):
                dve.wait_ge(bpe_lg, g + 1)
                ge(dve, b_rest, g - 1)
                parts = Lg[:, 0:2 * GB * E].rearrange("p (b w e) -> p b w e", b=GB, w=2)
                ge(dve, b_lg, g)
                dve.tensor_tensor(lg_part[:], parts[:, :, 1, :], br_bc[:].unsqueeze(1).broadcast_to([T, GB, E]), ALU.add) \
                   .then_inc(b_lg_part, 1)
                dve.wait_ge(b_lg_part, g + 1)
                dve.tensor_tensor(lg[r][:], lg_part[:], parts[:, :, 0, :], ALU.add).then_inc(b_lg, 1)
                dve.wait_ge(b_lg, g + 1)
                ge(dve, b_gap, g - 1)
                dve.tensor_reduce(top[r][:], lg[r][:], AX.X, ALU.max).then_inc(b_top, 1)
                dve.wait_ge(b_top, g + 1)
                ge(dve, b_rank2, g - 1)
                dve.tensor_tensor(eq[r][:], lg[r][:], bcast(top[r], E), ALU.is_equal).then_inc(b_eq, 1)
                dve.wait_ge(b_eq, g + 1)
                ge(dve, b_hot2, g - 1)
                dve.tensor_tensor(rank[r][:], eq[r][:], descend[:], ALU.mult).then_inc(b_rank, 1)
                dve.wait_ge(b_rank, g + 1)
                dve.tensor_reduce(best[r][:], rank[r][:], AX.X, ALU.max).then_inc(b_best, 1)
                dve.wait_ge(b_best, g + 1)
                ge(dve, b_hdif, g - 1)
                dve.tensor_tensor(hot1[r][:], rank[r][:], bcast(best[r], E), ALU.is_equal).then_inc(b_hot1, 1)
                dve.wait_ge(b_hot1, g + 1)
                ge(dve, b_eq2, g - 1)
                dve.scalar_tensor_tensor(rest[r][:], hot1[r][:], -BIG, lg[r][:], ALU.mult, ALU.add).then_inc(b_rest, 1)
                dve.wait_ge(b_rest, g + 1)
                dve.tensor_reduce(top2[r][:], rest[r][:], AX.X, ALU.max).then_inc(b_top2, 1)
                dve.wait_ge(b_top2, g + 1)
                dve.tensor_tensor(eq[r][:], rest[r][:], bcast(top2[r], E), ALU.is_equal).then_inc(b_eq2, 1)
                ge(dve, b_th, g - 1)
                dve.tensor_tensor(gap[r][:], top[r][:], top2[r][:], ALU.subtract).then_inc(b_gap, 1)
                dve.wait_ge(b_eq2, g + 1)
                dve.tensor_tensor(rank[r][:], eq[r][:], descend[:], ALU.mult).then_inc(b_rank2, 1)
                dve.wait_ge(b_rank2, g + 1)
                dve.tensor_reduce(best[r][:], rank[r][:], AX.X, ALU.max).then_inc(b_best2, 1)
                dve.wait_ge(b_best2, g + 1)
                ge(dve, b_w, g - 1)
                dve.tensor_tensor(hot2[r][:], rank[r][:], bcast(best[r], E), ALU.is_equal).then_inc(b_hot2, 1)

            def mix(g, b, r):
                s, q = 4 * g + b, b % 2
                dve.wait_ge(bpe_y, s + 1)
                dve.wait_ge(b_w, g + 1)
                ge(dve, b_moe, s - 1)
                dve.tensor_tensor(prod[q][:], Y[q][:].rearrange("p (e c) -> p e c", e=E),
                                  wfull[r][:, b, :].unsqueeze(2).broadcast_to([T, E, C]), ALU.mult).then_inc(b_prod, 1)
                dve.wait_ge(b_prod, s + 1)
                if b == 0:
                    ge(dve, b_final, g - 1)
                dve.tensor_reduce(moe[r][:, b, :], prod[q][:].rearrange("p e c -> p c e"), AX.X, ALU.add) \
                   .then_inc(b_moe, 1)

            def expert_step(k, par):
                opp = 1 - par
                if live(k):
                    dve.wait_ge(s_h1, 2 * (k + 1) if isinstance(k, int) else 2 * k + 2)
                    ge(dve, b_nmean, k - 1)
                    dve.tensor_reduce(hsum[par][:], resid[:, bass.ds(k * GB, GB), :], AX.X, ALU.add).then_inc(b_hsum, 1)
                    dve.wait_ge(b_hsum, k + 1)
                    ge(dve, b_xc, k - 1)
                    dve.tensor_scalar(nmean[par][:], hsum[par][:], -1.0 / C, None, ALU.mult).then_inc(b_nmean, 1)
                if live(k - 3):
                    mix(k - 3, 0, opp)
                if live(k - 1):
                    dve.wait_ge(b_xT, k)
                    ge(dve, bpe_l1, 8 * (k - 2))
                    dve.tensor_copy(xs2[opp][:], xT[opp][:]).then_inc(b_xhi, 1)
                    dve.wait_ge(b_xhi, k)
                    dve.tensor_tensor(xs2[opp][C:128], xT[opp][C:128], xs2[opp][C:128].bitcast(F32),
                                      ALU.subtract).then_inc(b_xs, 1)
                if live(k - 3):
                    mix(k - 3, 1, opp)
                if live(k):
                    dve.wait_ge(b_sq, k + 1)
                    ge(dve, b_var, k - 1)
                    dve.tensor_reduce(vsum[par][:], sq[par][:], AX.X, ALU.add).then_inc(b_vsum, 1)
                    ge(dve, b_rstd, k - 1)
                    dve.wait_ge(b_vsum, k + 1)
                    dve.tensor_scalar(var[par][:], vsum[par][:], (1.0 + EPS_LN) / C, EPS_LN ** 2, ALU.mult, ALU.add) \
                       .then_inc(b_var, 1)
                if live(k - 1):
                    route(k - 1, opp)
                if live(k - 3):
                    mix(k - 3, 2, opp)
                if live(k):
                    dve.wait_ge(b_rstd, k + 1)
                    ge(dve, bpe_d, k - 1)
                    dve.tensor_tensor(xn[par][:], xc[par][:].unsqueeze(2).broadcast_to([T, GB, 2, C]),
                                      rstd[par][:].unsqueeze(2).unsqueeze(3).broadcast_to([T, GB, 2, C]),
                                      ALU.mult).then_inc(b_xn, 1)
                if live(k - 3):
                    mix(k - 3, 3, opp)
                if live(k - 2):
                    dve.wait_ge(bpe_yb, k - 1)
                    ge(dve, b_final, k - 3)
                    dve.tensor_tensor(base[par][:], Wb[:, 0:GB * C].rearrange("p (b c) -> p b c", b=GB),
                                      resid[:, bass.ds((k - 2) * GB, GB), :], ALU.add).then_inc(b_base, 1)

            sweep(dve, expert_step, LOOP_B, STEPS_B)


def kernel(x, L0_tok_emb_table, L0_tok_W_in, L0_tok_b_oah, L0_attn_w_qkv, L0_attn_w_out, L0_attn_b_out,
           L0_ffn_gamma, L0_ffn_beta, L0_ffn_Wr, L0_ffn_br, L0_ffn_W1, L0_ffn_b1, L0_ffn_W2, L0_ffn_b2):
    import numpy as np
    import concourse.bacc as bacc
    from concourse.bass_utils import run_bass_kernel_spmd

    emb = np.asarray(L0_tok_emb_table)
    emb_ext = emb[(T - np.arange(2 * T)) % VROWS]
    arrays = {
        "x_ids": x, "emb_ext": emb_ext, "w_in_t": np.asarray(L0_tok_W_in).T, "b_oah": L0_tok_b_oah,
        "w_qkv": L0_attn_w_qkv, "w_out_t": np.asarray(L0_attn_w_out).T, "b_out": L0_attn_b_out,
        "gamma": L0_ffn_gamma, "beta": L0_ffn_beta, "w_r": L0_ffn_Wr, "b_r": L0_ffn_br,
        "w1": L0_ffn_W1, "b1_t": np.asarray(L0_ffn_b1).T, "w2": L0_ffn_W2, "b2": L0_ffn_b2,
    }
    arrays = {name: np.ascontiguousarray(a) for name, a in arrays.items()}
    nc = bacc.Bacc("TRN2", target_bir_lowering=False, num_devices=1)
    args = [nc.dram_tensor(name, a.shape, mybir.dt.from_np(a.dtype), kind="ExternalInput").ap()
            for name, a in arrays.items()]
    out = nc.dram_tensor("out", (B, T, C), F32, kind="ExternalOutput").ap()
    build_program(nc, *args, out)
    r = run_bass_kernel_spmd(nc, [arrays], core_ids=[0])
    return r.results[0]["out"]
```

```python
from contextlib import ExitStack

import concourse.bass as bass
from concourse import mybir

F32 = mybir.dt.float32
F32R = mybir.dt.float32r
BF16 = mybir.dt.bfloat16
I32 = mybir.dt.int32
ALU = mybir.AluOpType
ACT = mybir.ActivationFunctionType
AX = mybir.AxisListType

B, T, C = 128, 128, 64
HEADS, DH = 4, 64
E, H = 8, 128
GB = 4
NG = B // GB
GT = GB * T
VROWS = T + 1
ROW = 3 * C // 2 + C
SCALE = DH ** -0.5
EPS_LN = 1e-5
EPS_NRM = 1e-12
BIG = 3.0e38


def live(unit, count=NG):
    return not isinstance(unit, int) or 0 <= unit < count


def ge(eng, sem, value):
    if not isinstance(value, int) or value > 0:
        eng.wait_ge(sem, value)


def build_program(nc, x, emb_ext, w_in_t, b_oah, w_qkv, w_out_t, b_out, gamma, beta, w_r, b_r,
                  w1, b1_t, w2, b2, out):
    with ExitStack() as ctx:
        def sb(name, shape, dt=F32):
            return ctx.enter_context(nc.sbuf_tensor(name, shape, dt))

        def ps(name):
            return ctx.enter_context(nc.psum_tensor(name, [128, 512], F32))

        def sem(name):
            return ctx.enter_context(nc.semaphore(name))

        def ring(name, shape, dt=F32, n=2):
            return [sb(f"{name}{i}", shape, dt) for i in range(n)]

        ident = sb("ident", [128, 128])
        causal = sb("causal", [T, T], BF16)
        ones_col = sb("ones_col", [128, 1])
        ones_bf = sb("ones_bf", [128, 1], BF16)
        minus_half = sb("minus_half", [128, GB])
        x_int = sb("x_int", [B, T], I32)
        x_flt = sb("x_flt", [B, T])
        key = sb("key", [T, B])
        maskT = sb("maskT", [T, B])
        start_f = sb("start_f", [1, B])
        start_i = sb("start_i", [1, B], I32)
        emb_f = sb("emb_f", [128, 2, C])
        emb_rest = sb("emb_rest", [128, 2, C])
        emb_tab = sb("emb_tab", [128, 2, ROW])
        emb0 = sb("emb0", [1, C])
        emb0_sq = sb("emb0_sq", [1, C])
        nrm0 = sb("nrm0", [128, B // 2])
        w_in_diag = sb("w_in_diag", [128, 2, C])
        b_oah_bc = sb("b_oah_bc", [128, C])
        b_out_bc = sb("b_out_bc", [128, C])
        qkv = sb("qkv", [DH, 3 * HEADS, 2, C])
        wo = sb("wo", [DH, HEADS, C])
        m_hi = sb("m_hi", [128, HEADS * C], F32R)
        m_lo = sb("m_lo", [128, HEADS * C], F32R)
        n_hi = sb("n_hi", [128, HEADS * C], F32R)
        n_lo = sb("n_lo", [128, HEADS * C], F32R)
        w1_f = sb("w1_f", [128, E, H])
        w1_hi = sb("w1_hi", [128, E, H], F32R)
        w1_lo = sb("w1_lo", [128, E, H], F32R)
        b1_sb = sb("b1_sb", [H, E])
        w2_sb = sb("w2_sb", [H, E, C])
        b2_diag = sb("b2_diag", [GB * E, GB * C])
        wr_f = sb("wr_f", [128, E])
        wr_split = sb("wr_split", [128, 2, E], F32R)
        br_bc = sb("br_bc", [128, E])
        gamma2 = sb("gamma2", [128, 1])
        beta2 = sb("beta2", [128, 1])
        descend = sb("descend", [128, GB, E])

        resid = sb("resid", [T, B, C])

        ids = ring("ids", [128, GT], I32)
        pe_rows = ring("pe_rows", [T, GB, ROW])
        rel = ring("rel", [T, GB, T], BF16)
        maskg = ring("maskg", [T, GB])
        n2 = ring("n2", [128, GB // 2])
        n2g = ring("n2g", [128, GB // 2])
        rn = ring("rn", [128, GB // 2])
        p1s = ring("p1s", [128, GB // 2 * T])
        cnt = ring("cnt", [T, GB])
        rcnt = ring("rcnt", [T, GB])
        h0 = ring("h0", [T, GB, C])
        hcur = ring("hcur", [T, GB, C])
        hsum = ring("hsum", [T, GB])
        nmean = ring("nmean", [T, GB])
        xc = ring("xc", [T, GB, C])
        sq = ring("sq", [T, GB, C])
        vsum = ring("vsum", [T, GB])
        var = ring("var", [T, GB])
        rstd = ring("rstd", [T, GB])
        xn = ring("xn", [T, GB, 2, C])
        xdiag = ring("xdiag", [128, GB, 2, T])
        xs = ring("xs", [128, GT], F32R)
        z = [ring(f"z{p}", [128, GT]) for p in range(2)]
        u = ring("u", [T, GB, HEADS, C + 1])
        nmax = ring("nmax", [T, HEADS])
        prob = ring("prob", [T, HEADS, T])
        probT = ring("probT", [T, HEADS, T])
        rden = ring("rden", [T, HEADS])
        onorm = ring("onorm", [T, 2, HEADS, C])
        heads2 = ring("heads2", [T, 2, 2, C])
        attn = ring("attn", [T, 2, C])

        xT = ring("xT", [128, GT])
        xs2 = ring("xs2", [128, GT], F32R)
        lg_part = sb("lg_part", [T, GB, E])
        lg = ring("lg", [T, GB, E])
        top = ring("top", [T, GB])
        top2 = ring("top2", [T, GB])
        eq = ring("eq", [T, GB, E])
        rank = ring("rank", [T, GB, E])
        best = ring("best", [T, GB])
        hot1 = ring("hot1", [T, GB, E])
        hot2 = ring("hot2", [T, GB, E])
        rest = ring("rest", [T, GB, E])
        gap = ring("gap", [T, GB])
        th = ring("th", [T, GB])
        half = sb("half", [T, GB])
        whalf = ring("whalf", [T, GB])
        wfirst = ring("wfirst", [T, GB])
        hdif = ring("hdif", [T, GB, E])
        hmul = ring("hmul", [T, GB, E])
        wfull = ring("wfull", [T, GB, E])
        wT = ring("wT", [GB * E, T])
        hT = ring("hT", [H, E, GT])
        base = ring("base", [T, GB, C])
        prod = ring("prod", [T, E, C])
        moe = ring("moe", [T, GB, C])
        yout = ring("yout", [T, GB, C])

        table = nc.dram_tensor("table", (256, ROW), F32, kind="Internal").ap()

        S = [ps("psS0"), ps("psS1")]
        PT = [ps("psT0"), ps("psT1")]
        O = [ps("psO0"), ps("psO1")]
        M = [ps("psM0"), ps("psM1")]

        s_ld_x, s_ld_emb, s_ld_att, s_ld_ffn = (sem(n) for n in ("ld_x", "ld_emb", "ld_att", "ld_ffn"))
        s_const, s_zero, s_one = sem("const"), sem("zero"), sem("one")
        s_causal = sem("causal_done")
        s_xflt, s_xT, s_keyT, s_len, s_start, s_startf = (sem(n) for n in ("xflt", "xTd", "keyT", "len", "start", "startf"))
        s_emb, s_table, s_e0, s_n0, s_nrm0 = (sem(n) for n in ("emb", "tabled", "e0", "n0", "nrm0d"))
        s_fold, s_split, s_w1 = sem("fold"), sem("split"), sem("w1split")
        s_b2z, s_w_in_zero = sem("b2z"), sem("w_in_zero")
        s_ids = [sem("ids_a"), sem("ids_b")]
        s_rows = [sem("rows_a"), sem("rows_b")]
        (s_rel, pe_n2, s_n2, s_n2g, s_rn, pe_p1, s_p1s, pe_o1, s_cnt, s_rcnt, s_h0, s_h, s_hsum, s_nmean,
         s_xc, s_sq, s_vsum, s_var, s_rstd, s_xn, s_base_h) = (
            sem(f"a_{n}") for n in ("rel", "pe_n2", "n2", "n2g", "rn", "pe_p1", "p1s", "pe_o1", "cnt", "rcnt", "h0",
                                    "h", "hsum", "nmean", "xc", "sq", "vsum", "var", "rstd", "xn", "base_h"))
        (pe_d, s_xdiag, s_xhi, s_xs, pe_z, s_z, pe_u01, pe_u23, s_u01, s_u23) = (
            sem(f"a_{n}") for n in ("pe_d", "xdiag", "xhi", "xs", "pe_z", "z", "pe_u01", "pe_u23", "u01", "u23"))
        (pe_dots, s_nmax, s_exp, pe_t, s_pt, pe_v, s_rden, s_on, s_attn, s_h1) = (
            sem(f"a_{n}") for n in ("pe_dots", "nmax", "exp", "pe_t", "pt", "pe_v", "rden", "on", "attn", "h1"))
        (b_hsum, b_nmean, b_xc, b_sq, b_vsum, b_var, b_rstd, b_xn, bpe_d, b_xT, b_xhi, b_xs) = (
            sem(f"b_{n}") for n in ("hsum", "nmean", "xc", "sq", "vsum", "var", "rstd", "xn", "pe_d", "xT", "xhi", "xs"))
        (bpe_lg, b_lg, b_top, b_eq, b_rank, b_best, b_hot1, b_rest, b_top2, b_eq2, b_rank2, b_best2, b_hot2,
         b_gap, b_th, b_wfirst, b_hdif, b_hmul, b_w, bpe_wT, b_wT, bpe_yb, b_base) = (
            sem(f"b_{n}") for n in ("pe_lg", "lg", "top", "eq", "rank", "best", "hot1", "rest", "top2", "eq2", "rank2",
                                    "best2", "hot2", "gap", "th", "wfirst", "hdif", "hmul", "w", "pe_wT", "wT",
                                    "pe_yb", "base"))
        (bpe_l1, b_gelu, bpe_y, b_prod, b_moe, b_final) = (
            sem(f"b_{n}") for n in ("pe_l1", "gelu", "pe_y", "prod", "moe", "out"))
        s_heads2, s_maskg = sem("a_heads2"), sem("a_maskg")
        b_whalf, b_lg_part = sem("b_whalf"), sem("b_lg_part")
        s_store = [sem("store_a"), sem("store_b")]

        block = ctx.enter_context(nc.Block())

        ids_flat = x.rearrange("b t -> (b t)")
        LOOP_A = (4, 30)
        STEPS_A = NG + 2
        LOOP_B = (4, 32)
        HALVES = (0, 64)
        FFN_LOADED = 16 * (11 + GB)
        STEPS_B = NG + 3

        def sweep(eng, step, loop, steps):
            for k in range(loop[0]):
                step(k, k % 2)
            with eng.Fori(loop[0] // 2, loop[1] // 2) as i:
                step(2 * i, 0)
                step(2 * i + 1, 1)
            for k in range(loop[1], steps):
                step(k, k % 2)

        @block.sync
        def _(sp):
            sp.dma_start(x_int[:], x).then_inc(s_ld_x, 16)
            sp.dma_start(emb_f[:], emb_ext.rearrange("(c p) n -> p c n", p=128)).then_inc(s_ld_emb, 16)
            sp.dma_start(emb0[:], emb_ext[T:T + 1, :]).then_inc(s_ld_emb, 16)
            for d in range(2):
                sp.dma_start(qkv[:, :, d, :], w_qkv.rearrange("(c e) d -> e c d", e=DH)).then_inc(s_ld_att, 16)
            sp.dma_start(wo[:], w_out_t.rearrange("(h e) o -> e h o", e=DH)).then_inc(s_ld_att, 16)
            sp.wait_ge(s_w_in_zero, 1)
            for d in range(2):
                sp.dma_start(w_in_diag[d * C:d * C + C, d], w_in_t).then_inc(s_ld_att, 16)
            sp.dma_start(b_oah_bc[:], b_oah.partition_broadcast(128)).then_inc(s_ld_att, 16)
            sp.dma_start(b_out_bc[:], b_out.partition_broadcast(128)).then_inc(s_ld_att, 16)
            sp.wait_ge(s_emb, 1)
            sp.dma_start(table.rearrange("(c p) n -> p c n", p=128), emb_tab[:]).then_inc(s_table, 16)
            sp.wait_ge(s_table, 16)
            sp.wait_ge(s_start, 1)

            def step(k, par):
                ge(sp, s_rel, k - 1)
                sp.dma_start(ids[par][:], ids_flat[bass.ds(k * GT, GT)].partition_broadcast(128)) \
                  .then_inc(s_ids[par], 16)
                ge(sp, pe_p1, k - 1)
                for b in range(GB):
                    first = sp.value_load(start_i[0:1, bass.ds(k * GB + b, 1)], min_val=0, max_val=T)
                    sp.dma_start(pe_rows[par][:, b, :], table[bass.ds(first, T), :]).then_inc(s_rows[par], 16)

            sweep(sp, step, (2, NG), NG)

            def store(k, par):
                ge(sp, b_final, k + 1)
                sp.dma_start(out[bass.ds(k * GB, GB)].rearrange("b t c -> t b c"), yout[par][:]) \
                  .then_inc(s_store[par], 16)

            sweep(sp, store, (2, NG), NG)
            for par in range(2):
                sp.wait_ge(s_store[par], 16 * NG // 2)

        @block.gpsimd
        def _(pool):
            pool.memset(ident[:], 0.0).then_inc(s_zero, 1)
            pool.memset(causal[:], 1.0).then_inc(s_one, 1)
            pool.wait_ge(s_zero, 1)
            pool.affine_select(out=ident[:], in_=ident[:], compare_op=ALU.not_equal, fill=1.0, base=0,
                               pattern=[[-1, 128]], channel_multiplier=1).then_inc(s_const, 1)
            pool.wait_ge(s_one, 1)
            pool.affine_select(out=causal[:], in_=causal[:], compare_op=ALU.is_ge, fill=0.0, base=0,
                               pattern=[[-1, T]], channel_multiplier=1).then_inc(s_causal, 1)
            pool.memset(b2_diag[:], 0.0).then_inc(s_b2z, 1)
            pool.dma_start(w1_f[0:C], w1.rearrange("e d h -> d e h")).then_inc(s_ld_ffn, 16)
            pool.dma_start(w1_f[C:128], w1.rearrange("e d h -> d e h")).then_inc(s_ld_ffn, 16)
            pool.dma_start(b1_sb[:], b1_t).then_inc(s_ld_ffn, 16)
            pool.dma_start(w2_sb[:], w2.rearrange("e h c -> h e c")).then_inc(s_ld_ffn, 16)
            pool.dma_start(br_bc[:], b_r.partition_broadcast(128)).then_inc(s_ld_ffn, 16)
            for d in range(2):
                pool.dma_start(wr_f[d * C:d * C + C], w_r).then_inc(s_ld_ffn, 16)
                pool.dma_start(gamma2[d * C:d * C + C], gamma.unsqueeze(1)).then_inc(s_ld_ffn, 16)
                pool.dma_start(beta2[d * C:d * C + C], beta.unsqueeze(1)).then_inc(s_ld_ffn, 16)
            pool.wait_ge(s_b2z, 1)
            for b in range(GB):
                pool.dma_start(b2_diag[b * E:b * E + E, b * C:b * C + C], b2).then_inc(s_ld_ffn, 16)

            pool.wait_ge(s_split, 1)
            pool.wait_ge(s_ld_att, 112)

            def add_pair(m_attn, col, par):
                ge(pool, s_on, 2 * m_attn + 2)
                ge(pool, s_attn, m_attn - 1)
                pool.tensor_tensor(heads2[par][:], onorm[par][:, :, 0:2, :], onorm[par][:, :, 2:4, :], ALU.add) \
                    .then_inc(s_heads2, 1)
                pool.wait_ge(s_heads2, m_attn + 1)
                ge(pool, s_h1, m_attn - 1)
                pool.tensor_tensor(attn[par][:], heads2[par][:, :, 0, :], heads2[par][:, :, 1, :], ALU.add) \
                    .then_inc(s_attn, 1)
                pool.wait_ge(s_attn, m_attn + 1)
                dst = resid[:, bass.ds(col, 2), :]
                pool.tensor_tensor(dst, dst, attn[par][:], ALU.add).then_inc(s_h1, 1)

            def mask_columns(k, par):
                ge(pool, pe_n2, k - 1)
                pool.tensor_copy(maskg[par][:], maskT[:, bass.ds(k * GB, GB)]).then_inc(s_maskg, 1)

            pool.wait_ge(s_keyT, 1)
            mask_columns(0, 0)

            def step(k, par):
                a = k - 2
                if live(k):
                    ge(pool, s_p1s, k - 1)
                    pool.wait_ge(s_n2g, k + 1)
                    pool.tensor_tensor(rn[par][:], n2g[par][:], minus_half[:, 0:GB // 2], ALU.pow).then_inc(s_rn, 1)
                if live(k + 1):
                    mask_columns(k + 1, 1 - par)
                if live(a - 1):
                    ge(pool, s_base_h, a)
                    add_pair(2 * (a - 1), (a - 1) * GB, 0)
                if live(k):
                    pool.wait_ge(s_h0, k + 1)
                    ge(pool, s_hsum, k - 1)
                    ge(pool, s_base_h, k - 1)
                    pool.tensor_tensor(hcur[par][:], h0[par][:], b_oah_bc[:].unsqueeze(1).broadcast_to([T, GB, C]),
                                       ALU.add).then_inc(s_h, 1)
                    pool.wait_ge(s_h, k + 1)
                    pool.tensor_tensor(resid[:, bass.ds(k * GB, GB), :], hcur[par][:],
                                       b_out_bc[:].unsqueeze(1).broadcast_to([T, GB, C]), ALU.add).then_inc(s_base_h, 1)
                    pool.wait_ge(s_nmean, k + 1)
                    ge(pool, s_xn, k - 1)
                    pool.tensor_tensor(xc[par][:], hcur[par][:], nmean[par][:].unsqueeze(2).broadcast_to([T, GB, C]),
                                       ALU.add).then_inc(s_xc, 1)
                    ge(pool, s_vsum, k - 1)
                    pool.wait_ge(s_xc, k + 1)
                    pool.tensor_tensor(sq[par][:], xc[par][:], xc[par][:], ALU.mult).then_inc(s_sq, 1)
                if live(k):
                    pool.wait_ge(s_var, k + 1)
                    pool.tensor_tensor(rstd[par][:], var[par][:], minus_half[:], ALU.pow).then_inc(s_rstd, 1)
                if live(a - 1):
                    add_pair(2 * (a - 1) + 1, (a - 1) * GB + 2, 1)

            sweep(pool, step, LOOP_A, STEPS_A + 1)

            def expert_step(k, par):
                opp = 1 - par
                if live(k):
                    pool.wait_ge(b_nmean, k + 1)
                    ge(pool, b_xn, k - 1)
                    pool.tensor_tensor(xc[par][:], resid[:, bass.ds(k * GB, GB), :],
                                       nmean[par][:].unsqueeze(2).broadcast_to([T, GB, C]), ALU.add).then_inc(b_xc, 1)
                    ge(pool, b_vsum, k - 1)
                    pool.wait_ge(b_xc, k + 1)
                    pool.tensor_tensor(sq[par][:], xc[par][:], xc[par][:], ALU.mult).then_inc(b_sq, 1)
                if live(k - 2):
                    g = k - 2
                    pool.wait_ge(b_th, g + 1)
                    pool.tensor_tensor(whalf[par][:], th[par][:], half[:], ALU.mult).then_inc(b_whalf, 1)
                    pool.wait_ge(b_whalf, g + 1)
                    ge(pool, b_hmul, g - 1)
                    pool.tensor_tensor(wfirst[par][:], whalf[par][:], half[:], ALU.add).then_inc(b_wfirst, 1)
                    pool.wait_ge(b_hot2, g + 1)
                    pool.tensor_tensor(hdif[par][:], hot1[par][:], hot2[par][:], ALU.subtract).then_inc(b_hdif, 1)
                    pool.wait_ge(b_hdif, g + 1)
                    pool.wait_ge(b_wfirst, g + 1)
                    pool.tensor_tensor(hmul[par][:], hdif[par][:],
                                       wfirst[par][:].unsqueeze(2).broadcast_to([T, GB, E]), ALU.mult).then_inc(b_hmul, 1)
                    ge(pool, b_prod, 4 * (g - 1))
                    ge(pool, bpe_wT, g - 1)
                    pool.wait_ge(b_hmul, g + 1)
                    pool.tensor_tensor(wfull[par][:], hmul[par][:], hot2[par][:], ALU.add).then_inc(b_w, 1)
                if live(k):
                    pool.wait_ge(b_var, k + 1)
                    pool.tensor_tensor(rstd[par][:], var[par][:], minus_half[:], ALU.pow).then_inc(b_rstd, 1)
                if live(k - 3):
                    g = k - 3
                    pool.wait_ge(b_moe, 4 * (g + 1))
                    pool.wait_ge(b_base, g + 1)
                    ge(pool, s_store[opp], 8 * (g - opp))
                    pool.tensor_tensor(yout[opp][:], moe[opp][:], base[opp][:], ALU.add).then_inc(b_final, 1)

            pool.wait_ge(s_xn, NG)
            sweep(pool, expert_step, LOOP_B, STEPS_B)

        @block.tensor
        def _(pe):
            pe.wait_ge(s_const, 1)
            pe.wait_ge(s_xflt, 1)
            pe.transpose(M[0][:, 0:B], x_flt[:], ident[:]).then_inc(s_xT, 1)
            pe.wait_ge(s_keyT, 2)
            pe.matmul(M[1][0:1, 0:B], ones_col[:], maskT[:], start=True, stop=True).then_inc(s_len, 1)
            pe.wait_ge(s_startf, 1)
            pe.wait_ge(s_e0, 1)
            starts = start_f[:].rearrange("o (m d) -> o d m", d=2)
            for d in range(2):
                last = pe.matmul(O[0][d * C:d * C + C, 0:B // 2], emb0_sq[:], starts[:, d], start=True, stop=True)
            last.then_inc(s_n0, 1)
            pe.wait_ge(s_ld_att, 112)
            for h in range(HEADS):
                pe.matmul(S[0][:, h * C:h * C + C], qkv[:, h, :, :], qkv[:, HEADS + h, 0, :], start=True, stop=True)
            for h in range(HEADS):
                last = pe.matmul(S[1][:, h * C:h * C + C], qkv[:, 2 * HEADS + h, :, :], wo[:, h, :],
                                 start=True, stop=True)
            last.then_inc(s_fold, 1)
            pe.wait_ge(s_split, 1)
            pe.wait_ge(s_nrm0, 1)
            pe.wait_ge(s_keyT, 3)

            def dots(s, b, par, a):
                q = b % 2
                if b == 0:
                    ge(pe, s_z, a + 1)
                ge(pe, s_exp, s - 1)
                for p in range(2):
                    last = pe.matmul(S[q][:, 2 * p * T:2 * p * T + 2 * T], z[p][par][:, b * T:b * T + T],
                                     xdiag[par][:, b, :, :], start=True, stop=True)
                last.then_inc(pe_dots, 1)

            def turn(s, q):
                ge(pe, s_exp, s + 1)
                ge(pe, s_pt, s - 1)
                for h in range(HEADS):
                    last = pe.transpose(PT[q][:, h * T:h * T + T], prob[q][:, h, :], ident[:])
                last.then_inc(pe_t, 1)

            def weigh(s, b, par, g):
                q = b % 2
                if b == 0:
                    ge(pe, s_u01, g + 1)
                    ge(pe, s_u23, g + 1)
                ge(pe, s_pt, s + 1)
                ge(pe, s_on, s - 1)
                for h in range(HEADS):
                    for t in HALVES:
                        last = pe.matmul(O[q][t:t + 64, h * (C + 1):(h + 1) * (C + 1)], probT[q][:, h, t:t + 64],
                                         u[par][:, b, h, :], start=True, stop=True)
                last.then_inc(pe_v, 1)

            def step(k, par):
                a, opp = k - 2, 1 - par
                if live(a):
                    dots(4 * a, 0, par, a)
                if live(k):
                    rows = pe_rows[par][:].bitcast(BF16)
                    pe.wait_ge(s_rows[par], 32 * (k - par) + 64)
                    pe.wait_ge(s_maskg, k + 1)
                    ge(pe, s_u01, k - 1)
                    for b in range(GB):
                        d = b % 2 * C
                        last = pe.matmul(M[1][d:d + C, b // 2:b // 2 + 1], pe_rows[par][:, b, 3 * C // 2:ROW],
                                         maskg[par][:, b:b + 1], start=True, stop=True)
                    last.then_inc(pe_n2, 1)
                    pe.wait_ge(s_rel, k + 1)
                    ge(pe, s_u23, k - 1)
                    ge(pe, s_h0, k)
                    for b in range(GB):
                        d, m = b % 2 * C, b // 2
                        for part in range(3):
                            last = pe.matmul(M[0][d:d + C, m * T:m * T + T], rows[:, b, part * C:part * C + C],
                                             rel[par][:, b, :], start=(part == 0), stop=(part == 2))
                    last.then_inc(pe_p1, 1)
                if live(a - 1):
                    turn(4 * a - 1, 1)
                    weigh(4 * a - 2, 2, opp, a - 1)
                if live(k - 1):
                    pe.wait_ge(s_xn, k)
                    ge(pe, s_n2, k + 1 if live(k) else 0)
                    for b in range(GB):
                        last = pe.transpose(M[1][:, b * T:b * T + T], xn[opp][:, b, :, :], ident[:])
                    last.then_inc(pe_d, 1)
                if live(a):
                    dots(4 * a + 1, 1, par, a)
                if live(a):
                    turn(4 * a, 0)
                if live(k):
                    pe.wait_ge(s_p1s, k + 1)
                    for b in range(GB):
                        pe.matmul(M[0][:, GB * C + b:GB * C + b + 1], rel[par][:, b, :], ones_bf[:], start=True, stop=True)
                    for m in range(GB // 2):
                        last = pe.matmul(M[0][:, m * 2 * C:(m + 1) * 2 * C], p1s[par][:, m * T:m * T + T], w_in_diag[:],
                                         start=True, stop=True)
                    last.then_inc(pe_o1, 1)
                if live(a - 1):
                    weigh(4 * a - 1, 3, opp, a - 1)
                if live(a):
                    dots(4 * a + 2, 2, par, a)
                    turn(4 * a + 1, 1)
                if live(k - 1):
                    pe.wait_ge(s_xs, k)
                    pe.wait_ge(s_xdiag, k)
                    ge(pe, s_h0, k + 1 if live(k) else 0)
                    for p in range(2):
                        bank = M[1 - p]
                        pe.matmul(bank[:], m_hi[:, p * 2 * C:(p + 1) * 2 * C], xs[opp][:], start=True, stop=False)
                        last = pe.matmul(bank[:], m_lo[:, p * 2 * C:(p + 1) * 2 * C], xs[opp][:], start=False, stop=True)
                    last.then_inc(pe_z, 1)
                if live(a):
                    weigh(4 * a, 0, par, a)
                if live(a):
                    dots(4 * a + 3, 3, par, a)
                    turn(4 * a + 2, 0)
                if live(k - 1):
                    pe.wait_ge(s_z, k)
                    for half, done in ((0, pe_u01), (1, pe_u23)):
                        bank = M[1 - half]
                        for b in range(2):
                            tok = (2 * half + b) * T
                            dst = bank[:, b * HEADS * C:(b + 1) * HEADS * C]
                            pe.matmul(dst, xs[opp][:, tok:tok + T], n_hi[:], start=True, stop=False)
                            last = pe.matmul(dst, xs[opp][:, tok:tok + T], n_lo[:], start=False, stop=True)
                        last.then_inc(done, 1)
                if live(a):
                    weigh(4 * a + 1, 1, par, a)

            sweep(pe, step, LOOP_A, STEPS_A + 1)

            pe.wait_ge(s_exp, B)
            pe.wait_ge(s_pt, B)
            pe.wait_ge(s_on, B)
            pe.wait_ge(s_u01, NG)
            pe.wait_ge(s_u23, NG)
            pe.wait_ge(s_ld_ffn, FFN_LOADED)
            pe.wait_ge(s_w1, 2)
            L, Y, Dp, Lg, Wb = S, O, PT[0], PT[1], M[0]

            def expert_step(k, par):
                opp = 1 - par
                for b in range(GB):
                    for e in (2 * b, 2 * b + 1):
                        if live(k - 2):
                            g, n = k - 2, 8 * (k - 2) + e
                            if e == 0:
                                pe.wait_ge(b_xs, g + 1)
                            ge(pe, b_gelu, n - 1)
                            pe.matmul(L[e % 2][:], w1_hi[:, e, :], xs2[par][:], start=True, stop=False)
                            pe.matmul(L[e % 2][:], w1_lo[:, e, :], xs2[par][:], start=False, stop=True).then_inc(bpe_l1, 1)
                    if b == 1 and live(k - 1):
                        pe.wait_ge(b_xn, k)
                        ge(pe, b_xT, k - 1)
                        for i in range(GB):
                            last = pe.transpose(Dp[:, i * T:i * T + T], xn[opp][:, i, :, :], ident[:])
                        last.then_inc(bpe_d, 1)
                    if live(k - 3):
                        g = k - 3
                        if b == 0:
                            pe.wait_ge(b_gelu, 8 * (g + 1))
                        ge(pe, b_prod, 4 * g + b - 1)
                        for e in range(E):
                            for t in HALVES:
                                last = pe.matmul(Y[b % 2][t:t + 64, e * C:e * C + C],
                                                 hT[opp][:, e, b * T + t:b * T + t + 64], w2_sb[:, e, :],
                                                 start=True, stop=True)
                        last.then_inc(bpe_y, 1)
                    if b == 2 and live(k - 1):
                        pe.wait_ge(b_xs, k)
                        ge(pe, b_lg, k - 1)
                        for i in range(GB):
                            last = pe.matmul(Lg[:, i * 2 * E:(i + 1) * 2 * E], xs2[opp][:, i * T:i * T + T], wr_split[:],
                                             start=True, stop=True)
                        last.then_inc(bpe_lg, 1)
                    if b == 2 and live(k - 2):
                        pe.wait_ge(b_w, k - 1)
                        ge(pe, b_base, k - 2)
                        pe.transpose(Wb[0:GB * E, 256:256 + T], wfull[par][:], ident[:]).then_inc(bpe_wT, 1)
                    if b == 3 and live(k - 2):
                        pe.wait_ge(b_wT, k - 1)
                        pe.matmul(Wb[:, 0:GB * C], wT[par][:], b2_diag[:], start=True, stop=True).then_inc(bpe_yb, 1)

            sweep(pe, expert_step, LOOP_B, STEPS_B)

        @block.scalar
        def _(act):
            def exps(s, q):
                ge(act, s_nmax, s + 1)
                ge(act, pe_t, s - 1)
                for h in range(HEADS):
                    last = act.activation(prob[q][:, h, :], S[q][:, h * T:h * T + T], ACT.Exp, bias=nmax[q][:, h:h + 1])
                last.then_inc(s_exp, 1)

            def take_turned(s, q):
                ge(act, pe_t, s + 1)
                ge(act, pe_v, s - 1)
                act.copy(probT[q][:], PT[q][:].rearrange("p (h i) -> p h i", h=HEADS)).then_inc(s_pt, 1)

            act.wait_ge(s_split, 1)

            def step(k, par):
                a, opp = k - 2, 1 - par
                if live(a):
                    exps(4 * a, 0)
                if live(a - 1):
                    take_turned(4 * a - 1, 1)
                if live(k - 1):
                    act.wait_ge(pe_d, k)
                    ge(act, pe_dots, 4 * (k - 2))
                    ge(act, s_xs, k - 2)
                    src = M[1][:].rearrange("p (b t) -> p b t", b=GB)
                    act.copy(xdiag[opp][0:C, :, 0, :], src[0:C])
                    act.copy(xdiag[opp][C:128, :, 1, :], src[C:128]).then_inc(s_xdiag, 1)
                if live(a):
                    exps(4 * a + 1, 1)
                if live(a):
                    take_turned(4 * a, 0)
                if live(a):
                    exps(4 * a + 2, 0)
                if live(k - 1):
                    act.wait_ge(pe_z, k)
                    ge(act, pe_dots, 4 * (k - 2))
                    act.copy(z[0][opp][:], M[1][:])
                    act.copy(z[1][opp][:], M[0][:]).then_inc(s_z, 1)
                if live(a):
                    take_turned(4 * a + 1, 1)
                if live(a):
                    exps(4 * a + 3, 1)
                if live(k - 1):
                    act.wait_ge(pe_u01, k)
                    ge(act, pe_v, 4 * (k - 2))
                    act.copy(u[opp][:, 0:2, :, 0:C], M[1][:].rearrange("p (b h c) -> p b h c", b=2, h=HEADS)) \
                       .then_inc(s_u01, 1)
                    act.wait_ge(pe_u23, k)
                    act.copy(u[opp][:, 2:4, :, 0:C], M[0][:].rearrange("p (b h c) -> p b h c", b=2, h=HEADS)) \
                       .then_inc(s_u23, 1)
                if live(a):
                    take_turned(4 * a + 2, 0)

            sweep(act, step, LOOP_A, STEPS_A + 1)

            act.wait_ge(s_ld_ffn, FFN_LOADED)

            def expert_step(k, par):
                opp = 1 - par
                for e in range(E):
                    if live(k - 2):
                        g, n = k - 2, 8 * (k - 2) + e
                        act.wait_ge(bpe_l1, n + 1)
                        if e % 2 == 0:
                            ge(act, bpe_y, 4 * (g - 1))
                        act.activation(hT[par][:, e, :], L[e % 2][:], ACT.Gelu, bias=b1_sb[:, e:e + 1]).then_inc(b_gelu, 1)
                    if e == 2 and live(k - 1):
                        act.wait_ge(bpe_d, k)
                        ge(act, b_xs, k - 2)
                        act.activation(xT[opp][:], Dp[:], ACT.Identity, scale=gamma2[:], bias=beta2[:]).then_inc(b_xT, 1)
                    if e == 3 and live(k - 2):
                        g = k - 2
                        act.wait_ge(b_gap, g + 1)
                        ge(act, b_wfirst, g - 1)
                        act.activation(th[par][:], gap[par][:], ACT.Tanh, scale=0.5).then_inc(b_th, 1)
                    if e == 6 and live(k - 2):
                        act.wait_ge(bpe_wT, k - 1)
                        ge(act, bpe_yb, k - 3)
                        act.copy(wT[par][:], Wb[0:GB * E, 256:256 + T]).then_inc(b_wT, 1)

            L, Dp, Wb = S, PT[0], M[0]
            sweep(act, expert_step, LOOP_B, STEPS_B)

        @block.vector
        def _(dve):
            dve.memset(ones_col[:], 1.0)
            dve.memset(ones_bf[:], 1.0)
            dve.memset(minus_half[:], -0.5)
            dve.memset(w_in_diag[:], 0.0).then_inc(s_w_in_zero, 1)
            dve.memset(half[:], 0.5)
            dve.memset(emb_tab[:], 0.0)
            for r in range(2):
                dve.memset(xdiag[r][:], 0.0)
                dve.memset(u[r][:, :, :, C:C + 1], 1.0)
            for w in (m_lo, n_lo):
                dve.memset(w[C:128].bitcast(F32), 0.0)
            dve.memset(w1_lo[C:128].bitcast(F32), 0.0)
            dve.memset(wr_split[C:128, 1].bitcast(F32), 0.0)
            for e in range(E):
                dve.memset(descend[:, :, e:e + 1], float(E - e))
            dve.wait_ge(s_ld_x, 16)
            dve.tensor_copy(x_flt[:], x_int[:]).then_inc(s_xflt, 1)
            dve.wait_ge(s_xT, 1)
            dve.tensor_scalar(maskT[:], M[0][:, 0:B], 0.0, None, ALU.not_equal).then_inc(s_keyT, 1)
            dve.tensor_scalar(key[:], M[0][:, 0:B], 0.0, -0.5, ALU.is_equal, ALU.mult).then_inc(s_keyT, 1)
            dve.wait_ge(s_keyT, 2)
            dve.tensor_tensor(key[:], key[:], M[0][:, 0:B], ALU.add).then_inc(s_keyT, 1)
            dve.wait_ge(s_len, 1)
            dve.tensor_scalar(start_f[:], M[1][0:1, 0:B], -1.0, float(T), ALU.mult, ALU.add).then_inc(s_startf, 1)
            dve.wait_ge(s_startf, 1)
            dve.tensor_copy(start_i[:], start_f[:]).then_inc(s_start, 1)
            chain = s_emb_chain = sem("emb_chain")
            dve.wait_ge(s_ld_emb, 32)
            dve.tensor_tensor(emb0_sq[:], emb0[:], emb0[:], ALU.mult).then_inc(s_e0, 1)
            parts = emb_tab[:].bitcast(BF16)
            dve.tensor_copy(parts[:, :, 0:C], emb_f[:]).then_inc(chain, 1)
            dve.tensor_tensor(emb_tab[:, :, 3 * C // 2:ROW], emb_f[:], emb_f[:], ALU.mult)
            dve.wait_ge(chain, 1)
            dve.tensor_tensor(emb_rest[:], emb_f[:], parts[:, :, 0:C], ALU.subtract).then_inc(chain, 1)
            dve.wait_ge(chain, 2)
            dve.tensor_copy(parts[:, :, C:2 * C], emb_rest[:]).then_inc(chain, 1)
            dve.wait_ge(chain, 3)
            dve.tensor_tensor(emb_rest[:], emb_rest[:], parts[:, :, C:2 * C], ALU.subtract).then_inc(chain, 1)
            dve.wait_ge(chain, 4)
            dve.tensor_copy(parts[:, :, 2 * C:3 * C], emb_rest[:]).then_inc(s_emb, 1)
            dve.wait_ge(s_n0, 1)
            dve.tensor_copy(nrm0[:], O[0][:, 0:B // 2]).then_inc(s_nrm0, 1)
            dve.wait_ge(s_fold, 1)
            dve.tensor_scalar(m_hi[:], S[0][:, 0:HEADS * C], SCALE, None, ALU.mult)
            dve.tensor_copy(n_hi[:], S[1][:, 0:HEADS * C]).then_inc(chain, 1)
            dve.wait_ge(chain, 5)
            dve.scalar_tensor_tensor(m_lo[0:C], S[0][0:C, 0:HEADS * C], SCALE, m_hi[0:C].bitcast(F32), ALU.mult, ALU.subtract)
            dve.tensor_tensor(n_lo[0:C], S[1][0:C, 0:HEADS * C], n_hi[0:C].bitcast(F32), ALU.subtract).then_inc(s_split, 1)

            def relation(k, par):
                dve.wait_ge(s_ids[par], 8 * (k - par) + 16)
                ge(dve, pe_o1, k - 1)
                for b in range(GB):
                    last = dve.scalar_tensor_tensor(rel[par][:, b, :], ids[par][:, b * T:b * T + T],
                                                    key[:, bass.ds(k * GB + b, 1)], causal[:], ALU.is_equal, ALU.mult)
                last.then_inc(s_rel, 1)

            def maxima(s, q):
                ge(dve, pe_dots, s + 1)
                ge(dve, s_exp, s - 1)
                dve.tensor_reduce(nmax[q][:], S[q][:].rearrange("p (h j) -> p h j", h=HEADS), AX.X, ALU.max,
                                  negate=True).then_inc(s_nmax, 1)

            def sums(s, b):
                q = b % 2
                ge(dve, pe_v, s + 1)
                ge(dve, s_on, s - 1)
                src = O[q][:, 0:HEADS * (C + 1)].rearrange("p (h c) -> p h c", h=HEADS)
                dve.reciprocal(rden[q][:], src[:, :, C]).then_inc(s_rden, 1)

            def divide(s, b, freed):
                q, m, half = b % 2, b // 2, b % 2
                src = O[q][:, 0:HEADS * (C + 1)].rearrange("p (h c) -> p h c", h=HEADS)
                if half == 0:
                    ge(dve, s_heads2, freed)
                ge(dve, s_rden, s + 1)
                dve.tensor_tensor(onorm[m][:, half], src[:, :, 0:C], rden[q][:].unsqueeze(2).broadcast_to([T, HEADS, C]),
                                  ALU.mult).then_inc(s_on, 1)

            dve.wait_ge(s_causal, 1)
            dve.wait_ge(s_keyT, 3)
            relation(0, 0)

            def step(k, par):
                a, opp = k - 2, 1 - par
                if live(a):
                    maxima(4 * a, 0)
                if live(k):
                    dve.wait_ge(pe_n2, k + 1)
                    dve.tensor_tensor(n2[par][:], M[1][:, 0:GB // 2], nrm0[:, bass.ds(k * (GB // 2), GB // 2)], ALU.add) \
                       .then_inc(s_n2, 1)
                if live(a - 1):
                    sums(4 * a - 3, 1)
                if live(k):
                    ge(dve, s_rn, k - 1)
                    dve.wait_ge(s_n2, k + 1)
                    dve.tensor_scalar(n2g[par][:], n2[par][:], EPS_NRM ** 2, None, ALU.max).then_inc(s_n2g, 1)
                if live(a - 1):
                    divide(4 * a - 3, 1, 0)
                    sums(4 * a - 2, 2)
                if live(a - 1):
                    divide(4 * a - 2, 2, 2 * a - 2)
                if live(k):
                    dve.wait_ge(pe_p1, k + 1)
                    dve.wait_ge(s_rn, k + 1)
                    ge(dve, pe_o1, k - 1)
                    dve.tensor_tensor(p1s[par][:].rearrange("p (m t) -> p m t", m=GB // 2),
                                      M[0][:, 0:GB // 2 * T].rearrange("p (m t) -> p m t", m=GB // 2),
                                      rn[par][:].unsqueeze(2).broadcast_to([128, GB // 2, T]), ALU.mult).then_inc(s_p1s, 1)
                if live(a):
                    maxima(4 * a + 1, 1)
                if live(k - 1):
                    dve.wait_ge(s_xdiag, k)
                    ge(dve, pe_u23, k - 2)
                    xs_v = xs[opp][:].rearrange("p (b t) -> p b t", b=GB)
                    dve.tensor_copy(xs_v[C:128], xdiag[opp][C:128, :, 1, :]).then_inc(s_xhi, 1)
                    dve.tensor_copy(xs_v[0:C], xdiag[opp][0:C, :, 0, :])
                    dve.wait_ge(s_xhi, k)
                    dve.tensor_tensor(xs_v[C:128], xdiag[opp][C:128, :, 1, :], xs_v[C:128].bitcast(F32),
                                      ALU.subtract).then_inc(s_xs, 1)
                if live(k):
                    dve.wait_ge(pe_o1, k + 1)
                    ge(dve, s_rcnt, k - 1)
                    dve.tensor_scalar(cnt[par][:], M[0][:, GB * C:GB * C + GB], 1.0, None, ALU.max).then_inc(s_cnt, 1)
                if live(a - 1):
                    sums(4 * a - 1, 3)
                if live(k):
                    ge(dve, s_h0, k - 1)
                    dve.wait_ge(s_cnt, k + 1)
                    dve.reciprocal(rcnt[par][:], cnt[par][:]).then_inc(s_rcnt, 1)
                    dve.wait_ge(s_rcnt, k + 1)
                    ge(dve, s_h, k - 1)
                    dve.tensor_tensor(h0[par][:], M[0][:, 0:GB * C].rearrange("p (b c) -> p b c", b=GB),
                                      rcnt[par][:].unsqueeze(2).broadcast_to([T, GB, C]), ALU.mult).then_inc(s_h0, 1)
                if live(a - 1):
                    divide(4 * a - 1, 3, 0)
                if live(a):
                    maxima(4 * a + 2, 0)
                if live(k):
                    dve.wait_ge(s_h, k + 1)
                    ge(dve, s_nmean, k - 1)
                    dve.tensor_reduce(hsum[par][:], hcur[par][:], AX.X, ALU.add).then_inc(s_hsum, 1)
                if live(k):
                    ge(dve, s_xc, k - 1)
                    dve.wait_ge(s_hsum, k + 1)
                    dve.tensor_scalar(nmean[par][:], hsum[par][:], -1.0 / C, None, ALU.mult).then_inc(s_nmean, 1)
                if live(a):
                    sums(4 * a, 0)
                if live(a):
                    divide(4 * a, 0, 2 * a - 1)
                if live(a):
                    maxima(4 * a + 3, 1)
                if live(k):
                    dve.wait_ge(s_sq, k + 1)
                    ge(dve, s_var, k - 1)
                    dve.tensor_reduce(vsum[par][:], sq[par][:], AX.X, ALU.add).then_inc(s_vsum, 1)
                    ge(dve, s_rstd, k - 1)
                    dve.wait_ge(s_vsum, k + 1)
                    dve.tensor_scalar(var[par][:], vsum[par][:], 1.0 / C, EPS_LN, ALU.mult, ALU.add).then_inc(s_var, 1)
                if live(k + 1):
                    relation(k + 1, opp)
                if live(k):
                    ge(dve, pe_d, k - 1)
                    dve.wait_ge(s_rstd, k + 1)
                    dve.tensor_tensor(xn[par][:], xc[par][:].unsqueeze(2).broadcast_to([T, GB, 2, C]),
                                      rstd[par][:].unsqueeze(2).unsqueeze(3).broadcast_to([T, GB, 2, C]),
                                      ALU.mult).then_inc(s_xn, 1)

            sweep(dve, step, LOOP_A, STEPS_A + 1)

            dve.wait_ge(s_ld_ffn, FFN_LOADED)
            dve.tensor_copy(wr_split[:, 0], wr_f[:])
            dve.tensor_copy(w1_hi[:], w1_f[:]).then_inc(s_w1, 1)
            dve.wait_ge(s_w1, 1)
            dve.tensor_tensor(wr_split[0:C, 1], wr_f[0:C], wr_split[0:C, 0].bitcast(F32), ALU.subtract)
            dve.tensor_tensor(w1_lo[0:C], w1_f[0:C], w1_hi[0:C].bitcast(F32), ALU.subtract).then_inc(s_w1, 1)
            dve.wait_ge(s_rstd, NG)
            dve.wait_ge(pe_d, NG)
            L, Y, Dp, Lg, Wb = S, O, PT[0], PT[1], M[0]

            def bcast(t, n):
                return t[:].unsqueeze(2).broadcast_to([T, GB, n])

            def route_logits(g, r):
                dve.wait_ge(bpe_lg, g + 1)
                ge(dve, b_lg, g)
                parts = Lg[:, 0:2 * GB * E].rearrange("p (b w e) -> p b w e", b=GB, w=2)
                dve.tensor_tensor(lg_part[:], parts[:, :, 1, :], br_bc[:].unsqueeze(1).broadcast_to([T, GB, E]), ALU.add) \
                   .then_inc(b_lg_part, 1)

            def route_logits_sum(g, r):
                ge(dve, b_rest, g - 1)
                dve.wait_ge(b_lg_part, g + 1)
                parts = Lg[:, 0:2 * GB * E].rearrange("p (b w e) -> p b w e", b=GB, w=2)
                dve.tensor_tensor(lg[r][:], lg_part[:], parts[:, :, 0, :], ALU.add).then_inc(b_lg, 1)

            def route_top(g, r):
                ge(dve, b_gap, g - 1)
                dve.wait_ge(b_lg, g + 1)
                dve.tensor_reduce(top[r][:], lg[r][:], AX.X, ALU.max).then_inc(b_top, 1)

            def route_equal(g, r):
                ge(dve, b_rank2, g - 1)
                dve.wait_ge(b_top, g + 1)
                dve.tensor_tensor(eq[r][:], lg[r][:], bcast(top[r], E), ALU.is_equal).then_inc(b_eq, 1)

            def route_rank(g, r):
                ge(dve, b_hot2, g - 1)
                dve.wait_ge(b_eq, g + 1)
                dve.tensor_tensor(rank[r][:], eq[r][:], descend[:], ALU.mult).then_inc(b_rank, 1)

            def route_best(g, r):
                dve.wait_ge(b_rank, g + 1)
                dve.tensor_reduce(best[r][:], rank[r][:], AX.X, ALU.max).then_inc(b_best, 1)

            def route_hot(g, r):
                ge(dve, b_hdif, g - 1)
                dve.wait_ge(b_best, g + 1)
                dve.tensor_tensor(hot1[r][:], rank[r][:], bcast(best[r], E), ALU.is_equal).then_inc(b_hot1, 1)

            def route_rest(g, r):
                ge(dve, b_eq2, g - 1)
                dve.wait_ge(b_hot1, g + 1)
                dve.scalar_tensor_tensor(rest[r][:], hot1[r][:], -BIG, lg[r][:], ALU.mult, ALU.add).then_inc(b_rest, 1)

            def route_top2(g, r):
                dve.wait_ge(b_rest, g + 1)
                dve.tensor_reduce(top2[r][:], rest[r][:], AX.X, ALU.max).then_inc(b_top2, 1)

            def route_equal2(g, r):
                dve.wait_ge(b_top2, g + 1)
                dve.tensor_tensor(eq[r][:], rest[r][:], bcast(top2[r], E), ALU.is_equal).then_inc(b_eq2, 1)
                ge(dve, b_th, g - 1)
                dve.tensor_tensor(gap[r][:], top[r][:], top2[r][:], ALU.subtract).then_inc(b_gap, 1)

            def route_rank2(g, r):
                dve.wait_ge(b_eq2, g + 1)
                dve.tensor_tensor(rank[r][:], eq[r][:], descend[:], ALU.mult).then_inc(b_rank2, 1)

            def route_best2(g, r):
                dve.wait_ge(b_rank2, g + 1)
                dve.tensor_reduce(best[r][:], rank[r][:], AX.X, ALU.max).then_inc(b_best2, 1)

            def route_hot2(g, r):
                ge(dve, b_w, g - 1)
                dve.wait_ge(b_best2, g + 1)
                dve.tensor_tensor(hot2[r][:], rank[r][:], bcast(best[r], E), ALU.is_equal).then_inc(b_hot2, 1)

            def mix(g, b, r):
                s, q = 4 * g + b, b % 2
                dve.wait_ge(bpe_y, s + 1)
                dve.wait_ge(b_w, g + 1)
                ge(dve, b_moe, s - 1)
                dve.tensor_tensor(prod[q][:], Y[q][:].rearrange("p (e c) -> p e c", e=E),
                                  wfull[r][:, b, :].unsqueeze(2).broadcast_to([T, E, C]), ALU.mult).then_inc(b_prod, 1)

            def mix_sum(g, b, r):
                s, q = 4 * g + b, b % 2
                if b == 0:
                    ge(dve, b_final, g - 1)
                dve.wait_ge(b_prod, s + 1)
                dve.tensor_reduce(moe[r][:, b, :], prod[q][:].rearrange("p e c -> p c e"), AX.X, ALU.add) \
                   .then_inc(b_moe, 1)

            def expert_step(k, par):
                opp = 1 - par
                if live(k):
                    dve.wait_ge(s_h1, 2 * (k + 1) if isinstance(k, int) else 2 * k + 2)
                    ge(dve, b_nmean, k - 1)
                    dve.tensor_reduce(hsum[par][:], resid[:, bass.ds(k * GB, GB), :], AX.X, ALU.add).then_inc(b_hsum, 1)
                if live(k - 2):
                    route_rest(k - 2, par)
                if live(k):
                    ge(dve, b_xc, k - 1)
                    dve.wait_ge(b_hsum, k + 1)
                    dve.tensor_scalar(nmean[par][:], hsum[par][:], -1.0 / C, None, ALU.mult).then_inc(b_nmean, 1)
                if live(k - 2):
                    route_top2(k - 2, par)
                if live(k - 3):
                    mix(k - 3, 0, opp)
                if live(k - 2):
                    route_equal2(k - 2, par)
                if live(k - 3):
                    mix_sum(k - 3, 0, opp)
                if live(k - 2):
                    route_rank2(k - 2, par)
                if live(k - 1):
                    dve.wait_ge(b_xT, k)
                    ge(dve, bpe_l1, 8 * (k - 2))
                    dve.tensor_copy(xs2[opp][:], xT[opp][:]).then_inc(b_xhi, 1)
                if live(k - 2):
                    route_best2(k - 2, par)
                if live(k - 1):
                    dve.wait_ge(b_xhi, k)
                    dve.tensor_tensor(xs2[opp][C:128], xT[opp][C:128], xs2[opp][C:128].bitcast(F32),
                                      ALU.subtract).then_inc(b_xs, 1)
                if live(k - 2):
                    route_hot2(k - 2, par)
                if live(k - 3):
                    mix(k - 3, 1, opp)
                if live(k):
                    dve.wait_ge(b_sq, k + 1)
                    ge(dve, b_var, k - 1)
                    dve.tensor_reduce(vsum[par][:], sq[par][:], AX.X, ALU.add).then_inc(b_vsum, 1)
                if live(k - 3):
                    mix_sum(k - 3, 1, opp)
                if live(k):
                    ge(dve, b_rstd, k - 1)
                    dve.wait_ge(b_vsum, k + 1)
                    dve.tensor_scalar(var[par][:], vsum[par][:], (1.0 + EPS_LN) / C, EPS_LN ** 2, ALU.mult, ALU.add) \
                       .then_inc(b_var, 1)
                if live(k - 1):
                    route_logits(k - 1, opp)
                if live(k - 3):
                    mix(k - 3, 2, opp)
                if live(k - 1):
                    route_logits_sum(k - 1, opp)
                if live(k - 3):
                    mix_sum(k - 3, 2, opp)
                if live(k - 1):
                    route_top(k - 1, opp)
                if live(k):
                    dve.wait_ge(b_rstd, k + 1)
                    ge(dve, bpe_d, k - 1)
                    dve.tensor_tensor(xn[par][:], xc[par][:].unsqueeze(2).broadcast_to([T, GB, 2, C]),
                                      rstd[par][:].unsqueeze(2).unsqueeze(3).broadcast_to([T, GB, 2, C]),
                                      ALU.mult).then_inc(b_xn, 1)
                if live(k - 1):
                    route_equal(k - 1, opp)
                if live(k - 3):
                    mix(k - 3, 3, opp)
                if live(k - 1):
                    route_rank(k - 1, opp)
                if live(k - 3):
                    mix_sum(k - 3, 3, opp)
                if live(k - 1):
                    route_best(k - 1, opp)
                if live(k - 2):
                    dve.wait_ge(bpe_yb, k - 1)
                    ge(dve, b_final, k - 3)
                    dve.tensor_tensor(base[par][:], Wb[:, 0:GB * C].rearrange("p (b c) -> p b c", b=GB),
                                      resid[:, bass.ds((k - 2) * GB, GB), :], ALU.add).then_inc(b_base, 1)
                if live(k - 1):
                    route_hot(k - 1, opp)

            sweep(dve, expert_step, LOOP_B, STEPS_B)


def kernel(x, L0_tok_emb_table, L0_tok_W_in, L0_tok_b_oah, L0_attn_w_qkv, L0_attn_w_out, L0_attn_b_out,
           L0_ffn_gamma, L0_ffn_beta, L0_ffn_Wr, L0_ffn_br, L0_ffn_W1, L0_ffn_b1, L0_ffn_W2, L0_ffn_b2):
    import numpy as np
    import concourse.bacc as bacc
    from concourse.bass_utils import run_bass_kernel_spmd

    emb = np.asarray(L0_tok_emb_table)
    emb_ext = emb[(T - np.arange(2 * T)) % VROWS]
    arrays = {
        "x_ids": x, "emb_ext": emb_ext, "w_in_t": np.asarray(L0_tok_W_in).T, "b_oah": L0_tok_b_oah,
        "w_qkv": L0_attn_w_qkv, "w_out_t": np.asarray(L0_attn_w_out).T, "b_out": L0_attn_b_out,
        "gamma": L0_ffn_gamma, "beta": L0_ffn_beta, "w_r": L0_ffn_Wr, "b_r": L0_ffn_br,
        "w1": L0_ffn_W1, "b1_t": np.asarray(L0_ffn_b1).T, "w2": L0_ffn_W2, "b2": L0_ffn_b2,
    }
    arrays = {name: np.ascontiguousarray(a) for name, a in arrays.items()}
    nc = bacc.Bacc("TRN2", target_bir_lowering=False, num_devices=1)
    args = [nc.dram_tensor(name, a.shape, mybir.dt.from_np(a.dtype), kind="ExternalInput").ap()
            for name, a in arrays.items()]
    out = nc.dram_tensor("out", (B, T, C), F32, kind="ExternalOutput").ap()
    build_program(nc, *args, out)
    r = run_bass_kernel_spmd(nc, [arrays], core_ids=[0])
    return r.results[0]["out"]
```

```python
from contextlib import ExitStack

import concourse.bass as bass
from concourse import mybir

F32 = mybir.dt.float32
F32R = mybir.dt.float32r
BF16 = mybir.dt.bfloat16
I32 = mybir.dt.int32
ALU = mybir.AluOpType
ACT = mybir.ActivationFunctionType
AX = mybir.AxisListType

B, T, C = 128, 128, 64
HEADS, DH = 4, 64
E, H = 8, 128
GB = 4
NG = B // GB
GT = GB * T
VROWS = T + 1
ROW = 3 * C // 2 + C
SCALE = DH ** -0.5
EPS_LN = 1e-5
EPS_NRM = 1e-12
BIG = 3.0e38


def live(unit, count=NG):
    return not isinstance(unit, int) or 0 <= unit < count


def at(k, *steps):
    return isinstance(k, int) and k in steps


def ge(eng, sem, value):
    if not isinstance(value, int) or value > 0:
        eng.wait_ge(sem, value)


def build_program(nc, x, emb_ext, w_in_t, b_oah, w_qkv, w_out_t, b_out, gamma, beta, w_r, b_r,
                  w1, b1_t, w2, b2, out):
    with ExitStack() as ctx:
        def sb(name, shape, dt=F32):
            return ctx.enter_context(nc.sbuf_tensor(name, shape, dt))

        def ps(name):
            return ctx.enter_context(nc.psum_tensor(name, [128, 512], F32))

        def sem(name):
            return ctx.enter_context(nc.semaphore(name))

        def ring(name, shape, dt=F32, n=2):
            return [sb(f"{name}{i}", shape, dt) for i in range(n)]

        ident = sb("ident", [128, 128])
        causal = sb("causal", [T, T], BF16)
        ones_col = sb("ones_col", [128, 1])
        ones_bf = sb("ones_bf", [128, 1], BF16)
        minus_half = sb("minus_half", [128, GB])
        x_int = sb("x_int", [B, T], I32)
        x_flt = sb("x_flt", [B, T])
        key = sb("key", [T, B])
        maskT = sb("maskT", [T, B])
        start_f = sb("start_f", [1, B])
        start_i = sb("start_i", [1, B], I32)
        emb_f = sb("emb_f", [128, 2, C])
        emb_rest = sb("emb_rest", [128, 2, C])
        emb_tab = sb("emb_tab", [128, 2, ROW])
        emb0 = sb("emb0", [1, C])
        emb0_sq = sb("emb0_sq", [1, C])
        nrm0 = sb("nrm0", [128, B // 2])
        w_in_diag = sb("w_in_diag", [128, 2, C])
        b_oah_bc = sb("b_oah_bc", [128, C])
        b_out_bc = sb("b_out_bc", [128, C])
        qkv = sb("qkv", [DH, 3 * HEADS, 2, C])
        wo = sb("wo", [DH, HEADS, C])
        m_hi = sb("m_hi", [128, HEADS * C], F32R)
        m_lo = sb("m_lo", [128, HEADS * C], F32R)
        n_hi = sb("n_hi", [128, HEADS * C], F32R)
        n_lo = sb("n_lo", [128, HEADS * C], F32R)
        w1_f = sb("w1_f", [128, E, H])
        w1_hi = sb("w1_hi", [128, E, H], F32R)
        w1_lo = sb("w1_lo", [128, E, H], F32R)
        b1_sb = sb("b1_sb", [H, E])
        w2_sb = sb("w2_sb", [H, E, C])
        b2_diag = sb("b2_diag", [GB * E, GB * C])
        wr_f = sb("wr_f", [128, E])
        wr_split = sb("wr_split", [128, 2, E], F32R)
        br_bc = sb("br_bc", [128, E])
        gamma2 = sb("gamma2", [128, 1])
        beta2 = sb("beta2", [128, 1])
        descend = sb("descend", [128, GB, E])

        resid = sb("resid", [T, B, C])

        ids = ring("ids", [128, GT], I32)
        pe_rows = ring("pe_rows", [T, GB, ROW])
        rel = ring("rel", [T, GB, T], BF16)
        maskg = ring("maskg", [T, GB])
        n2 = ring("n2", [128, GB // 2])
        n2g = ring("n2g", [128, GB // 2])
        rn = ring("rn", [128, GB // 2])
        p1s = ring("p1s", [128, GB // 2 * T])
        cnt = ring("cnt", [T, GB])
        rcnt = ring("rcnt", [T, GB])
        h0 = ring("h0", [T, GB, C])
        hcur = ring("hcur", [T, GB, C])
        hsum = ring("hsum", [T, GB])
        nmean = ring("nmean", [T, GB])
        xc = ring("xc", [T, GB, C])
        sq = ring("sq", [T, GB, C])
        vsum = ring("vsum", [T, GB])
        var = ring("var", [T, GB])
        rstd = ring("rstd", [T, GB])
        xn = ring("xn", [T, GB, 2, C])
        xdiag = ring("xdiag", [128, GB, 2, T])
        xs = ring("xs", [128, GT], F32R)
        z = [ring(f"z{p}", [128, GT]) for p in range(2)]
        u = ring("u", [T, GB, HEADS, C + 1])
        nmax = ring("nmax", [T, HEADS])
        prob = ring("prob", [T, HEADS, T])
        probT = ring("probT", [T, HEADS, T])
        rden = ring("rden", [T, HEADS])
        onorm = ring("onorm", [T, 2, HEADS, C])
        heads2 = ring("heads2", [T, 2, 2, C])
        attn = ring("attn", [T, 2, C])

        xT = ring("xT", [128, GT])
        xs2 = ring("xs2", [128, GT], F32R)
        lg_part = sb("lg_part", [T, GB, E])
        lg = ring("lg", [T, GB, E])
        top = ring("top", [T, GB])
        top2 = ring("top2", [T, GB])
        eq = ring("eq", [T, GB, E])
        rank = ring("rank", [T, GB, E])
        best = ring("best", [T, GB])
        hot1 = ring("hot1", [T, GB, E])
        hot2 = ring("hot2", [T, GB, E])
        rest = ring("rest", [T, GB, E])
        gap = ring("gap", [T, GB])
        th = ring("th", [T, GB])
        warm = sb("warm", [128, 1])
        half = sb("half", [T, GB])
        whalf = ring("whalf", [T, GB])
        wfirst = ring("wfirst", [T, GB])
        hdif = ring("hdif", [T, GB, E])
        hmul = ring("hmul", [T, GB, E])
        wfull = ring("wfull", [T, GB, E])
        wT = ring("wT", [GB * E, T])
        hT = ring("hT", [H, E, GT])
        base = ring("base", [T, GB, C])
        prod = ring("prod", [T, E, C])
        moe = ring("moe", [T, GB, C])
        yout = ring("yout", [T, GB, C])

        table = nc.dram_tensor("table", (256, ROW), F32, kind="Internal").ap()

        S = [ps("psS0"), ps("psS1")]
        PT = [ps("psT0"), ps("psT1")]
        O = [ps("psO0"), ps("psO1")]
        M = [ps("psM0"), ps("psM1")]

        s_ld_x, s_ld_emb, s_ld_att, s_ld_ffn = (sem(n) for n in ("ld_x", "ld_emb", "ld_att", "ld_ffn"))
        s_const, s_zero, s_one = sem("const"), sem("zero"), sem("one")
        s_causal = sem("causal_done")
        s_xflt, s_xT, s_keyT, s_len, s_start, s_startf = (sem(n) for n in ("xflt", "xTd", "keyT", "len", "start", "startf"))
        s_emb, s_table, s_e0, s_n0, s_nrm0 = (sem(n) for n in ("emb", "tabled", "e0", "n0", "nrm0d"))
        s_fold, s_split, s_w1 = sem("fold"), sem("split"), sem("w1split")
        s_fixed, s_emb_chain, s_split_hi = sem("fixed"), sem("emb_chain"), sem("split_hi")
        s_b2z, s_w_in_zero = sem("b2z"), sem("w_in_zero")
        s_ids = [sem("ids_a"), sem("ids_b")]
        s_rows = [sem("rows_a"), sem("rows_b")]
        (s_rel, pe_n2, s_n2, s_n2g, s_rn, pe_p1, s_p1s, pe_o1, s_cnt, s_rcnt, s_h0, s_h, s_hsum, s_nmean,
         s_xc, s_sq, s_vsum, s_var, s_rstd, s_xn, s_base_h) = (
            sem(f"a_{n}") for n in ("rel", "pe_n2", "n2", "n2g", "rn", "pe_p1", "p1s", "pe_o1", "cnt", "rcnt", "h0",
                                    "h", "hsum", "nmean", "xc", "sq", "vsum", "var", "rstd", "xn", "base_h"))
        (pe_d, s_xdiag, s_xhi, s_xs, pe_z, s_z, pe_u01, pe_u23, s_u01, s_u23) = (
            sem(f"a_{n}") for n in ("pe_d", "xdiag", "xhi", "xs", "pe_z", "z", "pe_u01", "pe_u23", "u01", "u23"))
        (pe_dots, s_nmax, s_exp, pe_t, s_pt, pe_v, s_rden, s_on, s_attn, s_h1) = (
            sem(f"a_{n}") for n in ("pe_dots", "nmax", "exp", "pe_t", "pt", "pe_v", "rden", "on", "attn", "h1"))
        (b_hsum, b_nmean, b_xc, b_sq, b_vsum, b_var, b_rstd, b_xn, bpe_d, b_xT, b_xhi, b_xs) = (
            sem(f"b_{n}") for n in ("hsum", "nmean", "xc", "sq", "vsum", "var", "rstd", "xn", "pe_d", "xT", "xhi", "xs"))
        (bpe_lg, b_lg, b_top, b_eq, b_rank, b_best, b_hot1, b_rest, b_top2, b_eq2, b_rank2, b_best2, b_hot2,
         b_gap, b_th, b_wfirst, b_hdif, b_hmul, b_w, bpe_wT, b_wT, bpe_yb, b_base) = (
            sem(f"b_{n}") for n in ("pe_lg", "lg", "top", "eq", "rank", "best", "hot1", "rest", "top2", "eq2", "rank2",
                                    "best2", "hot2", "gap", "th", "wfirst", "hdif", "hmul", "w", "pe_wT", "wT",
                                    "pe_yb", "base"))
        (bpe_l1, b_gelu, bpe_y, b_prod, b_moe, b_final) = (
            sem(f"b_{n}") for n in ("pe_l1", "gelu", "pe_y", "prod", "moe", "out"))
        s_heads2, s_maskg = sem("a_heads2"), sem("a_maskg")
        b_whalf, b_lg_part = sem("b_whalf"), sem("b_lg_part")
        s_store = [sem("store_a"), sem("store_b")]

        block = ctx.enter_context(nc.Block())

        ids_flat = x.rearrange("b t -> (b t)")
        LOOP_A = (4, 30)
        LOOP_B = (4, 32)
        HALVES = (0, 64)
        FFN_LOADED = 16 * (11 + GB)
        L, Y, Dp, Lg, Wb = S, O, M[1], M[0], PT[0]

        def steps(step, first, end):
            for k in range(first, end):
                step(k, k % 2)

        def looped(eng, step, loop):
            with eng.Fori(loop[0] // 2, loop[1] // 2) as i:
                step(2 * i, 0)
                step(2 * i + 1, 1)

        def sweeps(eng, attention_step, expert_step, handover):
            steps(attention_step, 0, LOOP_A[0])
            looped(eng, attention_step, LOOP_A)
            steps(attention_step, LOOP_A[1], NG + 3)
            handover()
            steps(expert_step, 2, LOOP_B[0])
            looped(eng, expert_step, LOOP_B)
            steps(expert_step, LOOP_B[1], NG + 3)

        @block.sync
        def _(sp):
            sp.dma_start(x_int[:], x).then_inc(s_ld_x, 16)
            sp.dma_start(emb_f[:], emb_ext.rearrange("(c p) n -> p c n", p=128)).then_inc(s_ld_emb, 16)
            sp.dma_start(emb0[:], emb_ext[T:T + 1, :]).then_inc(s_ld_emb, 16)
            for d in range(2):
                sp.dma_start(qkv[:, :, d, :], w_qkv.rearrange("(c e) d -> e c d", e=DH)).then_inc(s_ld_att, 16)
            sp.dma_start(wo[:], w_out_t.rearrange("(h e) o -> e h o", e=DH)).then_inc(s_ld_att, 16)
            sp.wait_ge(s_w_in_zero, 1)
            for d in range(2):
                sp.dma_start(w_in_diag[d * C:d * C + C, d], w_in_t).then_inc(s_ld_att, 16)
            sp.dma_start(b_oah_bc[:], b_oah.partition_broadcast(128)).then_inc(s_ld_att, 16)
            sp.dma_start(b_out_bc[:], b_out.partition_broadcast(128)).then_inc(s_ld_att, 16)
            sp.wait_ge(s_emb, 1)
            sp.dma_start(table.rearrange("(c p) n -> p c n", p=128), emb_tab[:]).then_inc(s_table, 16)
            sp.wait_ge(s_table, 16)
            sp.wait_ge(s_start, 1)

            def step(k, par):
                ge(sp, s_rel, k - 1)
                sp.dma_start(ids[par][:], ids_flat[bass.ds(k * GT, GT)].partition_broadcast(128)) \
                  .then_inc(s_ids[par], 16)
                ge(sp, pe_p1, k - 1)
                for b in range(GB):
                    first = sp.value_load(start_i[0:1, bass.ds(k * GB + b, 1)], min_val=0, max_val=T)
                    sp.dma_start(pe_rows[par][:, b, :], table[bass.ds(first, T), :]).then_inc(s_rows[par], 16)

            steps(step, 0, 2)
            looped(sp, step, (2, NG))

            def store(k, par):
                ge(sp, b_final, k + 1)
                sp.dma_start(out[bass.ds(k * GB, GB)].rearrange("b t c -> t b c"), yout[par][:]) \
                  .then_inc(s_store[par], 16)

            steps(store, 0, 2)
            looped(sp, store, (2, NG))
            for par in range(2):
                sp.wait_ge(s_store[par], 16 * NG // 2)

        @block.gpsimd
        def _(pool):
            pool.memset(ident[:], 0.0).then_inc(s_zero, 1)
            pool.memset(causal[:], 1.0).then_inc(s_one, 1)
            pool.wait_ge(s_zero, 1)
            pool.affine_select(out=ident[:], in_=ident[:], compare_op=ALU.not_equal, fill=1.0, base=0,
                               pattern=[[-1, 128]], channel_multiplier=1).then_inc(s_const, 1)
            pool.wait_ge(s_one, 1)
            pool.affine_select(out=causal[:], in_=causal[:], compare_op=ALU.is_ge, fill=0.0, base=0,
                               pattern=[[-1, T]], channel_multiplier=1).then_inc(s_causal, 1)
            pool.memset(b2_diag[:], 0.0).then_inc(s_b2z, 1)
            for r in range(2):
                pool.memset(xdiag[r][:], 0.0)
                pool.memset(u[r][:, :, :, C:C + 1], 1.0)
            for w in (m_lo, n_lo):
                pool.memset(w[:].bitcast(F32), 0.0)
            pool.memset(w1_lo[:].bitcast(F32), 0.0)
            pool.memset(wr_split[:].bitcast(F32), 0.0)
            for e in range(E):
                last = pool.memset(descend[:, :, e:e + 1], float(E - e))
            last.then_inc(s_fixed, 1)

            pool.wait_ge(s_w_in_zero, 1)
            pool.wait_ge(s_ld_att, 112)

            def add_pair(m_attn, col, par):
                ge(pool, s_on, 2 * m_attn + 2)
                ge(pool, s_attn, m_attn - 1)
                pool.tensor_tensor(heads2[par][:], onorm[par][:, :, 0:2, :], onorm[par][:, :, 2:4, :], ALU.add) \
                    .then_inc(s_heads2, 1)
                pool.wait_ge(s_heads2, m_attn + 1)
                ge(pool, s_h1, m_attn - 1)
                pool.tensor_tensor(attn[par][:], heads2[par][:, :, 0, :], heads2[par][:, :, 1, :], ALU.add) \
                    .then_inc(s_attn, 1)
                pool.wait_ge(s_attn, m_attn + 1)
                dst = resid[:, bass.ds(col, 2), :]
                pool.tensor_tensor(dst, dst, attn[par][:], ALU.add).then_inc(s_h1, 1)

            def mask_columns(k, par):
                ge(pool, pe_n2, k - 1)
                pool.tensor_copy(maskg[par][:], maskT[:, bass.ds(k * GB, GB)]).then_inc(s_maskg, 1)

            pool.wait_ge(s_keyT, 1)
            mask_columns(0, 0)

            def squares(k, par):
                if at(k, 0):
                    pool.wait_ge(s_xn, NG)
                pool.wait_ge(b_nmean, k + 1)
                ge(pool, b_xn, k - 1)
                pool.tensor_tensor(xc[par][:], resid[:, bass.ds(k * GB, GB), :],
                                   nmean[par][:].unsqueeze(2).broadcast_to([T, GB, C]), ALU.add).then_inc(b_xc, 1)
                ge(pool, b_vsum, k - 1)
                pool.wait_ge(b_xc, k + 1)
                pool.tensor_tensor(sq[par][:], xc[par][:], xc[par][:], ALU.mult).then_inc(b_sq, 1)

            def inverse_deviation(k, par):
                pool.wait_ge(b_var, k + 1)
                pool.tensor_tensor(rstd[par][:], var[par][:], minus_half[:], ALU.pow).then_inc(b_rstd, 1)

            def step(k, par):
                a = k - 2
                if live(k):
                    ge(pool, s_p1s, k - 1)
                    pool.wait_ge(s_n2g, k + 1)
                    pool.tensor_tensor(rn[par][:], n2g[par][:], minus_half[:, 0:GB // 2], ALU.pow).then_inc(s_rn, 1)
                if live(k + 1):
                    mask_columns(k + 1, 1 - par)
                if live(a - 1):
                    ge(pool, s_base_h, a)
                    add_pair(2 * (a - 1), (a - 1) * GB, 0)
                if live(k):
                    pool.wait_ge(s_h0, k + 1)
                    ge(pool, s_hsum, k - 1)
                    ge(pool, s_base_h, k - 1)
                    pool.tensor_tensor(hcur[par][:], h0[par][:], b_oah_bc[:].unsqueeze(1).broadcast_to([T, GB, C]),
                                       ALU.add).then_inc(s_h, 1)
                    pool.wait_ge(s_h, k + 1)
                    pool.tensor_tensor(resid[:, bass.ds(k * GB, GB), :], hcur[par][:],
                                       b_out_bc[:].unsqueeze(1).broadcast_to([T, GB, C]), ALU.add).then_inc(s_base_h, 1)
                    pool.wait_ge(s_nmean, k + 1)
                    ge(pool, s_xn, k - 1)
                    pool.tensor_tensor(xc[par][:], hcur[par][:], nmean[par][:].unsqueeze(2).broadcast_to([T, GB, C]),
                                       ALU.add).then_inc(s_xc, 1)
                    ge(pool, s_vsum, k - 1)
                    pool.wait_ge(s_xc, k + 1)
                    pool.tensor_tensor(sq[par][:], xc[par][:], xc[par][:], ALU.mult).then_inc(s_sq, 1)
                if live(k):
                    pool.wait_ge(s_var, k + 1)
                    pool.tensor_tensor(rstd[par][:], var[par][:], minus_half[:], ALU.pow).then_inc(s_rstd, 1)
                if at(k, NG, NG + 1):
                    squares(k - NG, par)
                    inverse_deviation(k - NG, par)
                if live(a - 1):
                    add_pair(2 * (a - 1) + 1, (a - 1) * GB + 2, 1)

            def expert_step(k, par):
                opp = 1 - par
                if live(k):
                    squares(k, par)
                if live(k - 2):
                    g = k - 2
                    pool.wait_ge(b_th, g + 1)
                    pool.tensor_tensor(whalf[par][:], th[par][:], half[:], ALU.mult).then_inc(b_whalf, 1)
                    pool.wait_ge(b_whalf, g + 1)
                    ge(pool, b_hmul, g - 1)
                    pool.tensor_tensor(wfirst[par][:], whalf[par][:], half[:], ALU.add).then_inc(b_wfirst, 1)
                    pool.wait_ge(b_hot2, g + 1)
                    pool.tensor_tensor(hdif[par][:], hot1[par][:], hot2[par][:], ALU.subtract).then_inc(b_hdif, 1)
                    pool.wait_ge(b_hdif, g + 1)
                    pool.wait_ge(b_wfirst, g + 1)
                    pool.tensor_tensor(hmul[par][:], hdif[par][:],
                                       wfirst[par][:].unsqueeze(2).broadcast_to([T, GB, E]), ALU.mult).then_inc(b_hmul, 1)
                    ge(pool, b_prod, 4 * (g - 1))
                    ge(pool, bpe_wT, g - 1)
                    pool.wait_ge(b_hmul, g + 1)
                    pool.tensor_tensor(wfull[par][:], hmul[par][:], hot2[par][:], ALU.add).then_inc(b_w, 1)
                if live(k):
                    inverse_deviation(k, par)
                if live(k - 3):
                    g = k - 3
                    pool.wait_ge(b_moe, 4 * (g + 1))
                    pool.wait_ge(b_base, g + 1)
                    ge(pool, s_store[opp], 8 * (g - opp))
                    pool.tensor_tensor(yout[opp][:], moe[opp][:], base[opp][:], ALU.add).then_inc(b_final, 1)

            def handover():
                pass

            sweeps(pool, step, expert_step, handover)

        @block.tensor
        def _(pe):
            pe.wait_ge(s_const, 1)
            pe.wait_ge(s_xflt, 1)
            pe.transpose(M[0][:, 0:B], x_flt[:], ident[:]).then_inc(s_xT, 1)
            pe.wait_ge(s_keyT, 1)
            pe.matmul(M[1][0:1, 0:B], ones_col[:], maskT[:], start=True, stop=True).then_inc(s_len, 1)
            pe.wait_ge(s_startf, 1)
            pe.wait_ge(s_e0, 1)
            starts = start_f[:].rearrange("o (m d) -> o d m", d=2)
            for d in range(2):
                last = pe.matmul(O[0][d * C:d * C + C, 0:B // 2], emb0_sq[:], starts[:, d], start=True, stop=True)
            last.then_inc(s_n0, 1)
            pe.wait_ge(s_ld_att, 112)
            for h in range(HEADS):
                pe.matmul(S[0][:, h * C:h * C + C], qkv[:, h, :, :], qkv[:, HEADS + h, 0, :], start=True, stop=True)
            for h in range(HEADS):
                last = pe.matmul(S[1][:, h * C:h * C + C], qkv[:, 2 * HEADS + h, :, :], wo[:, h, :],
                                 start=True, stop=True)
            last.then_inc(s_fold, 1)
            pe.wait_ge(s_nrm0, 1)
            pe.wait_ge(s_fixed, 1)
            pe.wait_ge(s_keyT, 3)

            def dots(s, b, par, a):
                q = b % 2
                if b == 0:
                    ge(pe, s_z, a + 1)
                ge(pe, s_exp, s - 1)
                for p in range(2):
                    last = pe.matmul(S[q][:, 2 * p * T:2 * p * T + 2 * T], z[p][par][:, b * T:b * T + T],
                                     xdiag[par][:, b, :, :], start=True, stop=True)
                last.then_inc(pe_dots, 1)

            def turn(s, q):
                ge(pe, s_exp, s + 1)
                ge(pe, s_pt, s - 1)
                for h in range(HEADS):
                    last = pe.transpose(PT[q][:, h * T:h * T + T], prob[q][:, h, :], ident[:])
                last.then_inc(pe_t, 1)

            def weigh(s, b, par, g):
                q = b % 2
                if b == 0:
                    ge(pe, s_u01, g + 1)
                    ge(pe, s_u23, g + 1)
                ge(pe, s_pt, s + 1)
                ge(pe, s_on, s - 1)
                for h in range(HEADS):
                    for t in HALVES:
                        last = pe.matmul(O[q][t:t + 64, h * (C + 1):(h + 1) * (C + 1)], probT[q][:, h, t:t + 64],
                                         u[par][:, b, h, :], start=True, stop=True)
                last.then_inc(pe_v, 1)

            def turn_x(g, r):
                if at(g, 0):
                    pe.wait_ge(s_u01, NG)
                pe.wait_ge(b_xn, g + 1)
                ge(pe, b_xT, g)
                for i in range(GB):
                    last = pe.transpose(Dp[:, i * T:i * T + T], xn[r][:, i, :, :], ident[:])
                last.then_inc(bpe_d, 1)

            def logits(g, r):
                if at(g, 0):
                    pe.wait_ge(s_u23, NG)
                    pe.wait_ge(s_ld_ffn, FFN_LOADED)
                    pe.wait_ge(s_w1, 2)
                pe.wait_ge(b_xs, g + 1)
                ge(pe, b_lg, g)
                for i in range(GB):
                    last = pe.matmul(Lg[:, i * 2 * E:(i + 1) * 2 * E], xs2[r][:, i * T:i * T + T], wr_split[:],
                                     start=True, stop=True)
                last.then_inc(bpe_lg, 1)

            def step(k, par):
                a, opp = k - 2, 1 - par
                if live(a):
                    dots(4 * a, 0, par, a)
                if live(k):
                    rows = pe_rows[par][:].bitcast(BF16)
                    pe.wait_ge(s_rows[par], 32 * (k - par) + 64)
                    pe.wait_ge(s_maskg, k + 1)
                    ge(pe, s_u01, k - 1)
                    for b in range(GB):
                        d = b % 2 * C
                        last = pe.matmul(M[1][d:d + C, b // 2:b // 2 + 1], pe_rows[par][:, b, 3 * C // 2:ROW],
                                         maskg[par][:, b:b + 1], start=True, stop=True)
                    last.then_inc(pe_n2, 1)
                    pe.wait_ge(s_rel, k + 1)
                    ge(pe, s_u23, k - 1)
                    ge(pe, s_h0, k)
                    for b in range(GB):
                        d, m = b % 2 * C, b // 2
                        for part in range(3):
                            last = pe.matmul(M[0][d:d + C, m * T:m * T + T], rows[:, b, part * C:part * C + C],
                                             rel[par][:, b, :], start=(part == 0), stop=(part == 2))
                    last.then_inc(pe_p1, 1)
                if live(a - 1):
                    turn(4 * a - 1, 1)
                    weigh(4 * a - 2, 2, opp, a - 1)
                if live(k - 1):
                    pe.wait_ge(s_xn, k)
                    ge(pe, s_n2, k + 1 if live(k) else 0)
                    for b in range(GB):
                        last = pe.transpose(M[1][:, b * T:b * T + T], xn[opp][:, b, :, :], ident[:])
                    last.then_inc(pe_d, 1)
                if at(k, NG + 1):
                    turn_x(0, opp)
                if live(a):
                    dots(4 * a + 1, 1, par, a)
                if live(a):
                    turn(4 * a, 0)
                if live(k):
                    pe.wait_ge(s_p1s, k + 1)
                    for b in range(GB):
                        pe.matmul(M[0][:, GB * C + b:GB * C + b + 1], rel[par][:, b, :], ones_bf[:], start=True, stop=True)
                    for m in range(GB // 2):
                        last = pe.matmul(M[0][:, m * 2 * C:(m + 1) * 2 * C], p1s[par][:, m * T:m * T + T], w_in_diag[:],
                                         start=True, stop=True)
                    last.then_inc(pe_o1, 1)
                if live(a - 1):
                    weigh(4 * a - 1, 3, opp, a - 1)
                if live(a):
                    dots(4 * a + 2, 2, par, a)
                    turn(4 * a + 1, 1)
                if live(k - 1):
                    if at(k, 1):
                        pe.wait_ge(s_split, 1)
                    pe.wait_ge(s_xs, k)
                    pe.wait_ge(s_xdiag, k)
                    ge(pe, s_h0, k + 1 if live(k) else 0)
                    for p in range(2):
                        bank = M[1 - p]
                        pe.matmul(bank[:], m_hi[:, p * 2 * C:(p + 1) * 2 * C], xs[opp][:], start=True, stop=False)
                        last = pe.matmul(bank[:], m_lo[:, p * 2 * C:(p + 1) * 2 * C], xs[opp][:], start=False, stop=True)
                    last.then_inc(pe_z, 1)
                if live(a):
                    weigh(4 * a, 0, par, a)
                if at(k, NG + 1):
                    logits(0, opp)
                if live(a):
                    dots(4 * a + 3, 3, par, a)
                    turn(4 * a + 2, 0)
                if live(k - 1):
                    pe.wait_ge(s_z, k)
                    for half, done in ((0, pe_u01), (1, pe_u23)):
                        bank = M[1 - half]
                        for b in range(2):
                            tok = (2 * half + b) * T
                            dst = bank[:, b * HEADS * C:(b + 1) * HEADS * C]
                            pe.matmul(dst, xs[opp][:, tok:tok + T], n_hi[:], start=True, stop=False)
                            last = pe.matmul(dst, xs[opp][:, tok:tok + T], n_lo[:], start=False, stop=True)
                        last.then_inc(done, 1)
                if live(a):
                    weigh(4 * a + 1, 1, par, a)

            def expert_step(k, par):
                opp = 1 - par
                for b in range(GB):
                    for e in (2 * b, 2 * b + 1):
                        if live(k - 2):
                            g, n = k - 2, 8 * (k - 2) + e
                            if e == 0:
                                pe.wait_ge(b_xs, g + 1)
                            ge(pe, b_gelu, n - 1)
                            pe.matmul(L[e % 2][:], w1_hi[:, e, :], xs2[par][:], start=True, stop=False)
                            pe.matmul(L[e % 2][:], w1_lo[:, e, :], xs2[par][:], start=False, stop=True).then_inc(bpe_l1, 1)
                    if b == 1 and live(k - 1):
                        turn_x(k - 1, opp)
                    if live(k - 3):
                        g = k - 3
                        if b == 0:
                            pe.wait_ge(b_gelu, 8 * (g + 1))
                        ge(pe, b_prod, 4 * g + b - 1)
                        for e in range(E):
                            for t in HALVES:
                                last = pe.matmul(Y[b % 2][t:t + 64, e * C:e * C + C],
                                                 hT[opp][:, e, b * T + t:b * T + t + 64], w2_sb[:, e, :],
                                                 start=True, stop=True)
                        last.then_inc(bpe_y, 1)
                    if b == 2 and live(k - 1):
                        logits(k - 1, opp)
                    if b == 2 and live(k - 2):
                        pe.wait_ge(b_w, k - 1)
                        ge(pe, b_base, k - 2)
                        pe.transpose(Wb[0:GB * E, 256:256 + T], wfull[par][:], ident[:]).then_inc(bpe_wT, 1)
                    if b == 3 and live(k - 2):
                        pe.wait_ge(b_wT, k - 1)
                        pe.matmul(Wb[:, 0:GB * C], wT[par][:], b2_diag[:], start=True, stop=True).then_inc(bpe_yb, 1)

            def handover():
                pe.wait_ge(s_exp, B)
                pe.wait_ge(s_pt, B)
                pe.wait_ge(s_on, B)

            sweeps(pe, step, expert_step, handover)

        @block.scalar
        def _(act):
            act.wait_ge(s_w_in_zero, 1)
            act.activation(warm[:], minus_half[:, 0:1], ACT.Exp)
            act.wait_ge(s_table, 16)
            act.dma_start(w1_f[0:C], w1.rearrange("e d h -> d e h")).then_inc(s_ld_ffn, 16)
            act.dma_start(w1_f[C:128], w1.rearrange("e d h -> d e h")).then_inc(s_ld_ffn, 16)
            act.dma_start(b1_sb[:], b1_t).then_inc(s_ld_ffn, 16)
            act.dma_start(w2_sb[:], w2.rearrange("e h c -> h e c")).then_inc(s_ld_ffn, 16)
            act.dma_start(br_bc[:], b_r.partition_broadcast(128)).then_inc(s_ld_ffn, 16)
            for d in range(2):
                act.dma_start(wr_f[d * C:d * C + C], w_r).then_inc(s_ld_ffn, 16)
                act.dma_start(gamma2[d * C:d * C + C], gamma.unsqueeze(1)).then_inc(s_ld_ffn, 16)
                act.dma_start(beta2[d * C:d * C + C], beta.unsqueeze(1)).then_inc(s_ld_ffn, 16)
            act.wait_ge(s_b2z, 1)
            for b in range(GB):
                act.dma_start(b2_diag[b * E:b * E + E, b * C:b * C + C], b2).then_inc(s_ld_ffn, 16)
            act.wait_ge(s_fixed, 1)

            def exps(s, q):
                ge(act, s_nmax, s + 1)
                ge(act, pe_t, s - 1)
                for h in range(HEADS):
                    last = act.activation(prob[q][:, h, :], S[q][:, h * T:h * T + T], ACT.Exp, bias=nmax[q][:, h:h + 1])
                last.then_inc(s_exp, 1)

            def take_turned(s, q):
                ge(act, pe_t, s + 1)
                ge(act, pe_v, s - 1)
                act.copy(probT[q][:], PT[q][:].rearrange("p (h i) -> p h i", h=HEADS)).then_inc(s_pt, 1)

            def scale_x(g, r):
                if at(g, 0):
                    act.wait_ge(s_ld_ffn, FFN_LOADED)
                act.wait_ge(bpe_d, g + 1)
                ge(act, b_xs, g - 1)
                act.activation(xT[r][:], Dp[:], ACT.Identity, scale=gamma2[:], bias=beta2[:]).then_inc(b_xT, 1)

            def step(k, par):
                a, opp = k - 2, 1 - par
                if live(a):
                    exps(4 * a, 0)
                if live(a - 1):
                    take_turned(4 * a - 1, 1)
                if live(k - 1):
                    act.wait_ge(pe_d, k)
                    ge(act, pe_dots, 4 * (k - 2))
                    ge(act, s_xs, k - 2)
                    src = M[1][:].rearrange("p (b t) -> p b t", b=GB)
                    act.copy(xdiag[opp][0:C, :, 0, :], src[0:C])
                    act.copy(xdiag[opp][C:128, :, 1, :], src[C:128]).then_inc(s_xdiag, 1)
                if at(k, NG + 1):
                    scale_x(0, opp)
                if live(a):
                    exps(4 * a + 1, 1)
                if live(a):
                    take_turned(4 * a, 0)
                if live(a):
                    exps(4 * a + 2, 0)
                if live(k - 1):
                    act.wait_ge(pe_z, k)
                    ge(act, pe_dots, 4 * (k - 2))
                    act.copy(z[0][opp][:], M[1][:])
                    act.copy(z[1][opp][:], M[0][:]).then_inc(s_z, 1)
                if live(a):
                    take_turned(4 * a + 1, 1)
                if live(a):
                    exps(4 * a + 3, 1)
                if live(k - 1):
                    act.wait_ge(pe_u01, k)
                    ge(act, pe_v, 4 * (k - 2))
                    act.copy(u[opp][:, 0:2, :, 0:C], M[1][:].rearrange("p (b h c) -> p b h c", b=2, h=HEADS)) \
                       .then_inc(s_u01, 1)
                    act.wait_ge(pe_u23, k)
                    act.copy(u[opp][:, 2:4, :, 0:C], M[0][:].rearrange("p (b h c) -> p b h c", b=2, h=HEADS)) \
                       .then_inc(s_u23, 1)
                if live(a):
                    take_turned(4 * a + 2, 0)

            def expert_step(k, par):
                opp = 1 - par
                for e in range(E):
                    if live(k - 2):
                        g, n = k - 2, 8 * (k - 2) + e
                        act.wait_ge(bpe_l1, n + 1)
                        if e % 2 == 0:
                            ge(act, bpe_y, 4 * (g - 1))
                        act.activation(hT[par][:, e, :], L[e % 2][:], ACT.Gelu, bias=b1_sb[:, e:e + 1]).then_inc(b_gelu, 1)
                    if e == 2 and live(k - 1):
                        scale_x(k - 1, opp)
                    if e == 3 and live(k - 2):
                        g = k - 2
                        act.wait_ge(b_gap, g + 1)
                        ge(act, b_wfirst, g - 1)
                        act.activation(th[par][:], gap[par][:], ACT.Tanh, scale=0.5).then_inc(b_th, 1)
                    if e == 6 and live(k - 2):
                        act.wait_ge(bpe_wT, k - 1)
                        ge(act, bpe_yb, k - 3)
                        act.copy(wT[par][:], Wb[0:GB * E, 256:256 + T]).then_inc(b_wT, 1)

            def handover():
                pass

            sweeps(act, step, expert_step, handover)

        @block.vector
        def _(dve):
            dve.memset(ones_col[:], 1.0)
            dve.memset(ones_bf[:], 1.0)
            dve.memset(minus_half[:], -0.5)
            dve.memset(w_in_diag[:], 0.0).then_inc(s_w_in_zero, 1)
            dve.memset(half[:], 0.5)
            dve.wait_ge(s_ld_x, 16)
            dve.tensor_copy(x_flt[:], x_int[:]).then_inc(s_xflt, 1)
            dve.wait_ge(s_ld_emb, 32)
            parts = emb_tab[:].bitcast(BF16)
            dve.tensor_copy(parts[:, :, 0:C], emb_f[:]).then_inc(s_emb_chain, 1)
            dve.tensor_tensor(emb_tab[:, :, 3 * C // 2:ROW], emb_f[:], emb_f[:], ALU.mult)
            dve.wait_ge(s_emb_chain, 1)
            dve.tensor_tensor(emb_rest[:], emb_f[:], parts[:, :, 0:C], ALU.subtract).then_inc(s_emb_chain, 1)
            dve.tensor_tensor(emb0_sq[:], emb0[:], emb0[:], ALU.mult).then_inc(s_e0, 1)
            dve.wait_ge(s_emb_chain, 2)
            dve.tensor_copy(parts[:, :, C:2 * C], emb_rest[:]).then_inc(s_emb_chain, 1)
            dve.wait_ge(s_xT, 1)
            dve.tensor_scalar(maskT[:], M[0][:, 0:B], 0.0, None, ALU.not_equal).then_inc(s_keyT, 1)
            dve.wait_ge(s_emb_chain, 3)
            dve.tensor_tensor(emb_rest[:], emb_rest[:], parts[:, :, C:2 * C], ALU.subtract).then_inc(s_emb_chain, 1)
            dve.tensor_scalar(key[:], M[0][:, 0:B], 0.0, -0.5, ALU.is_equal, ALU.mult).then_inc(s_keyT, 1)
            dve.wait_ge(s_emb_chain, 4)
            dve.tensor_copy(parts[:, :, 2 * C:3 * C], emb_rest[:]).then_inc(s_emb, 1)
            dve.wait_ge(s_len, 1)
            dve.tensor_scalar(start_f[:], M[1][0:1, 0:B], -1.0, float(T), ALU.mult, ALU.add).then_inc(s_startf, 1)
            dve.wait_ge(s_keyT, 2)
            dve.tensor_tensor(key[:], key[:], M[0][:, 0:B], ALU.add).then_inc(s_keyT, 1)
            dve.wait_ge(s_startf, 1)
            dve.tensor_copy(start_i[:], start_f[:]).then_inc(s_start, 1)
            dve.wait_ge(s_n0, 1)
            dve.tensor_copy(nrm0[:], O[0][:, 0:B // 2]).then_inc(s_nrm0, 1)
            def relation(k, par):
                dve.wait_ge(s_ids[par], 8 * (k - par) + 16)
                ge(dve, pe_o1, k - 1)
                for b in range(GB):
                    last = dve.scalar_tensor_tensor(rel[par][:, b, :], ids[par][:, b * T:b * T + T],
                                                    key[:, bass.ds(k * GB + b, 1)], causal[:], ALU.is_equal, ALU.mult)
                last.then_inc(s_rel, 1)

            def maxima(s, q):
                ge(dve, pe_dots, s + 1)
                ge(dve, s_exp, s - 1)
                dve.tensor_reduce(nmax[q][:], S[q][:].rearrange("p (h j) -> p h j", h=HEADS), AX.X, ALU.max,
                                  negate=True).then_inc(s_nmax, 1)

            def sums(s, b):
                q = b % 2
                ge(dve, pe_v, s + 1)
                ge(dve, s_on, s - 1)
                src = O[q][:, 0:HEADS * (C + 1)].rearrange("p (h c) -> p h c", h=HEADS)
                dve.reciprocal(rden[q][:], src[:, :, C]).then_inc(s_rden, 1)

            def divide(s, b, freed):
                q, m, half = b % 2, b // 2, b % 2
                src = O[q][:, 0:HEADS * (C + 1)].rearrange("p (h c) -> p h c", h=HEADS)
                if half == 0:
                    ge(dve, s_heads2, freed)
                ge(dve, s_rden, s + 1)
                dve.tensor_tensor(onorm[m][:, half], src[:, :, 0:C], rden[q][:].unsqueeze(2).broadcast_to([T, HEADS, C]),
                                  ALU.mult).then_inc(s_on, 1)

            def bcast(t, n):
                return t[:].unsqueeze(2).broadcast_to([T, GB, n])

            def route_logits(g, r):
                dve.wait_ge(bpe_lg, g + 1)
                ge(dve, b_lg, g)
                parts = Lg[:, 0:2 * GB * E].rearrange("p (b w e) -> p b w e", b=GB, w=2)
                dve.tensor_tensor(lg_part[:], parts[:, :, 1, :], br_bc[:].unsqueeze(1).broadcast_to([T, GB, E]), ALU.add) \
                   .then_inc(b_lg_part, 1)

            def route_logits_sum(g, r):
                ge(dve, b_rest, g - 1)
                dve.wait_ge(b_lg_part, g + 1)
                parts = Lg[:, 0:2 * GB * E].rearrange("p (b w e) -> p b w e", b=GB, w=2)
                dve.tensor_tensor(lg[r][:], lg_part[:], parts[:, :, 0, :], ALU.add).then_inc(b_lg, 1)

            def route_top(g, r):
                ge(dve, b_gap, g - 1)
                dve.wait_ge(b_lg, g + 1)
                dve.tensor_reduce(top[r][:], lg[r][:], AX.X, ALU.max).then_inc(b_top, 1)

            def route_equal(g, r):
                ge(dve, b_rank2, g - 1)
                dve.wait_ge(b_top, g + 1)
                dve.tensor_tensor(eq[r][:], lg[r][:], bcast(top[r], E), ALU.is_equal).then_inc(b_eq, 1)

            def route_rank(g, r):
                ge(dve, b_hot2, g - 1)
                dve.wait_ge(b_eq, g + 1)
                dve.tensor_tensor(rank[r][:], eq[r][:], descend[:], ALU.mult).then_inc(b_rank, 1)

            def route_best(g, r):
                dve.wait_ge(b_rank, g + 1)
                dve.tensor_reduce(best[r][:], rank[r][:], AX.X, ALU.max).then_inc(b_best, 1)

            def route_hot(g, r):
                ge(dve, b_hdif, g - 1)
                dve.wait_ge(b_best, g + 1)
                dve.tensor_tensor(hot1[r][:], rank[r][:], bcast(best[r], E), ALU.is_equal).then_inc(b_hot1, 1)

            def route_rest(g, r):
                ge(dve, b_eq2, g - 1)
                dve.wait_ge(b_hot1, g + 1)
                dve.scalar_tensor_tensor(rest[r][:], hot1[r][:], -BIG, lg[r][:], ALU.mult, ALU.add).then_inc(b_rest, 1)

            def route_top2(g, r):
                dve.wait_ge(b_rest, g + 1)
                dve.tensor_reduce(top2[r][:], rest[r][:], AX.X, ALU.max).then_inc(b_top2, 1)

            def route_equal2(g, r):
                dve.wait_ge(b_top2, g + 1)
                dve.tensor_tensor(eq[r][:], rest[r][:], bcast(top2[r], E), ALU.is_equal).then_inc(b_eq2, 1)
                ge(dve, b_th, g - 1)
                dve.tensor_tensor(gap[r][:], top[r][:], top2[r][:], ALU.subtract).then_inc(b_gap, 1)

            def route_rank2(g, r):
                dve.wait_ge(b_eq2, g + 1)
                dve.tensor_tensor(rank[r][:], eq[r][:], descend[:], ALU.mult).then_inc(b_rank2, 1)

            def route_best2(g, r):
                dve.wait_ge(b_rank2, g + 1)
                dve.tensor_reduce(best[r][:], rank[r][:], AX.X, ALU.max).then_inc(b_best2, 1)

            def route_hot2(g, r):
                ge(dve, b_w, g - 1)
                dve.wait_ge(b_best2, g + 1)
                dve.tensor_tensor(hot2[r][:], rank[r][:], bcast(best[r], E), ALU.is_equal).then_inc(b_hot2, 1)

            def mix(g, b, r):
                s, q = 4 * g + b, b % 2
                dve.wait_ge(bpe_y, s + 1)
                dve.wait_ge(b_w, g + 1)
                ge(dve, b_moe, s - 1)
                dve.tensor_tensor(prod[q][:], Y[q][:].rearrange("p (e c) -> p e c", e=E),
                                  wfull[r][:, b, :].unsqueeze(2).broadcast_to([T, E, C]), ALU.mult).then_inc(b_prod, 1)

            def mix_sum(g, b, r):
                s, q = 4 * g + b, b % 2
                if b == 0:
                    ge(dve, b_final, g - 1)
                dve.wait_ge(b_prod, s + 1)
                dve.tensor_reduce(moe[r][:, b, :], prod[q][:].rearrange("p e c -> p c e"), AX.X, ALU.add) \
                   .then_inc(b_moe, 1)

            def ln_sum(k, par):
                if at(k, 0):
                    dve.wait_ge(s_rstd, NG)
                    dve.wait_ge(pe_d, NG)
                dve.wait_ge(s_h1, 2 * (k + 1) if isinstance(k, int) else 2 * k + 2)
                ge(dve, b_nmean, k - 1)
                dve.tensor_reduce(hsum[par][:], resid[:, bass.ds(k * GB, GB), :], AX.X, ALU.add).then_inc(b_hsum, 1)

            def ln_mean(k, par):
                ge(dve, b_xc, k - 1)
                dve.wait_ge(b_hsum, k + 1)
                dve.tensor_scalar(nmean[par][:], hsum[par][:], -1.0 / C, None, ALU.mult).then_inc(b_nmean, 1)

            def ln_square_sum(k, par):
                dve.wait_ge(b_sq, k + 1)
                ge(dve, b_var, k - 1)
                dve.tensor_reduce(vsum[par][:], sq[par][:], AX.X, ALU.add).then_inc(b_vsum, 1)

            def ln_variance(k, par):
                ge(dve, b_rstd, k - 1)
                dve.wait_ge(b_vsum, k + 1)
                dve.tensor_scalar(var[par][:], vsum[par][:], (1.0 + EPS_LN) / C, EPS_LN ** 2, ALU.mult, ALU.add) \
                   .then_inc(b_var, 1)

            def ln_normalise(k, par):
                dve.wait_ge(b_rstd, k + 1)
                ge(dve, bpe_d, k - 1)
                dve.tensor_tensor(xn[par][:], xc[par][:].unsqueeze(2).broadcast_to([T, GB, 2, C]),
                                  rstd[par][:].unsqueeze(2).unsqueeze(3).broadcast_to([T, GB, 2, C]),
                                  ALU.mult).then_inc(b_xn, 1)

            def x_high(g, r):
                dve.wait_ge(b_xT, g + 1)
                ge(dve, bpe_l1, 8 * (g - 1))
                dve.tensor_copy(xs2[r][:], xT[r][:]).then_inc(b_xhi, 1)

            def x_low(g, r):
                dve.wait_ge(b_xhi, g + 1)
                dve.tensor_tensor(xs2[r][C:128], xT[r][C:128], xs2[r][C:128].bitcast(F32), ALU.subtract).then_inc(b_xs, 1)

            dve.wait_ge(s_causal, 1)
            dve.wait_ge(s_keyT, 3)
            relation(0, 0)
            dve.wait_ge(s_fixed, 1)
            dve.wait_ge(s_fold, 1)
            dve.tensor_scalar(m_hi[:], S[0][:, 0:HEADS * C], SCALE, None, ALU.mult)
            dve.tensor_copy(n_hi[:], S[1][:, 0:HEADS * C]).then_inc(s_split_hi, 1)
            dve.wait_ge(s_split_hi, 1)
            dve.scalar_tensor_tensor(m_lo[0:C], S[0][0:C, 0:HEADS * C], SCALE, m_hi[0:C].bitcast(F32), ALU.mult, ALU.subtract)
            dve.tensor_tensor(n_lo[0:C], S[1][0:C, 0:HEADS * C], n_hi[0:C].bitcast(F32), ALU.subtract).then_inc(s_split, 1)
            def split_expert_weights():
                dve.wait_ge(s_ld_ffn, FFN_LOADED)
                dve.tensor_copy(wr_split[:, 0], wr_f[:])
                dve.tensor_copy(w1_hi[:], w1_f[:]).then_inc(s_w1, 1)
                dve.wait_ge(s_w1, 1)
                dve.tensor_tensor(wr_split[0:C, 1], wr_f[0:C], wr_split[0:C, 0].bitcast(F32), ALU.subtract)
                dve.tensor_tensor(w1_lo[0:C], w1_f[0:C], w1_hi[0:C].bitcast(F32), ALU.subtract).then_inc(s_w1, 1)

            def step(k, par):
                a, opp = k - 2, 1 - par
                if live(a):
                    maxima(4 * a, 0)
                if live(k):
                    dve.wait_ge(pe_n2, k + 1)
                    dve.tensor_tensor(n2[par][:], M[1][:, 0:GB // 2], nrm0[:, bass.ds(k * (GB // 2), GB // 2)], ALU.add) \
                       .then_inc(s_n2, 1)
                if live(a - 1):
                    sums(4 * a - 3, 1)
                if live(k):
                    ge(dve, s_rn, k - 1)
                    dve.wait_ge(s_n2, k + 1)
                    dve.tensor_scalar(n2g[par][:], n2[par][:], EPS_NRM ** 2, None, ALU.max).then_inc(s_n2g, 1)
                if live(a - 1):
                    divide(4 * a - 3, 1, 0)
                    sums(4 * a - 2, 2)
                if live(a - 1):
                    divide(4 * a - 2, 2, 2 * a - 2)
                if live(k):
                    dve.wait_ge(pe_p1, k + 1)
                    dve.wait_ge(s_rn, k + 1)
                    ge(dve, pe_o1, k - 1)
                    dve.tensor_tensor(p1s[par][:].rearrange("p (m t) -> p m t", m=GB // 2),
                                      M[0][:, 0:GB // 2 * T].rearrange("p (m t) -> p m t", m=GB // 2),
                                      rn[par][:].unsqueeze(2).broadcast_to([128, GB // 2, T]), ALU.mult).then_inc(s_p1s, 1)
                if live(a):
                    maxima(4 * a + 1, 1)
                if live(k - 1):
                    dve.wait_ge(s_xdiag, k)
                    ge(dve, pe_u23, k - 2)
                    xs_v = xs[opp][:].rearrange("p (b t) -> p b t", b=GB)
                    dve.tensor_copy(xs_v[C:128], xdiag[opp][C:128, :, 1, :]).then_inc(s_xhi, 1)
                    dve.tensor_copy(xs_v[0:C], xdiag[opp][0:C, :, 0, :])
                    dve.wait_ge(s_xhi, k)
                    dve.tensor_tensor(xs_v[C:128], xdiag[opp][C:128, :, 1, :], xs_v[C:128].bitcast(F32),
                                      ALU.subtract).then_inc(s_xs, 1)
                if at(k, NG + 1):
                    x_high(0, opp)
                    x_low(0, opp)
                if live(k):
                    dve.wait_ge(pe_o1, k + 1)
                    ge(dve, s_rcnt, k - 1)
                    dve.tensor_scalar(cnt[par][:], M[0][:, GB * C:GB * C + GB], 1.0, None, ALU.max).then_inc(s_cnt, 1)
                if live(a - 1):
                    sums(4 * a - 1, 3)
                if live(k):
                    ge(dve, s_h0, k - 1)
                    dve.wait_ge(s_cnt, k + 1)
                    dve.reciprocal(rcnt[par][:], cnt[par][:]).then_inc(s_rcnt, 1)
                    dve.wait_ge(s_rcnt, k + 1)
                    ge(dve, s_h, k - 1)
                    dve.tensor_tensor(h0[par][:], M[0][:, 0:GB * C].rearrange("p (b c) -> p b c", b=GB),
                                      rcnt[par][:].unsqueeze(2).broadcast_to([T, GB, C]), ALU.mult).then_inc(s_h0, 1)
                if live(a - 1):
                    divide(4 * a - 1, 3, 0)
                if live(a):
                    maxima(4 * a + 2, 0)
                if live(k):
                    dve.wait_ge(s_h, k + 1)
                    ge(dve, s_nmean, k - 1)
                    dve.tensor_reduce(hsum[par][:], hcur[par][:], AX.X, ALU.add).then_inc(s_hsum, 1)
                if live(k):
                    ge(dve, s_xc, k - 1)
                    dve.wait_ge(s_hsum, k + 1)
                    dve.tensor_scalar(nmean[par][:], hsum[par][:], -1.0 / C, None, ALU.mult).then_inc(s_nmean, 1)
                if at(k, NG, NG + 1):
                    ln_sum(k - NG, par)
                    ln_mean(k - NG, par)
                if live(a):
                    sums(4 * a, 0)
                if live(a):
                    divide(4 * a, 0, 2 * a - 1)
                if live(a):
                    maxima(4 * a + 3, 1)
                if at(k, NG + 1):
                    route_logits(0, opp)
                    route_logits_sum(0, opp)
                if at(k, NG, NG + 1):
                    ln_square_sum(k - NG, par)
                    ln_variance(k - NG, par)
                if at(k, NG + 1):
                    for stage in (route_top, route_equal, route_rank, route_best, route_hot):
                        stage(0, opp)
                if at(k, NG, NG + 1):
                    ln_normalise(k - NG, par)
                if at(k, 1):
                    split_expert_weights()
                if live(k):
                    dve.wait_ge(s_sq, k + 1)
                    ge(dve, s_var, k - 1)
                    dve.tensor_reduce(vsum[par][:], sq[par][:], AX.X, ALU.add).then_inc(s_vsum, 1)
                    ge(dve, s_rstd, k - 1)
                    dve.wait_ge(s_vsum, k + 1)
                    dve.tensor_scalar(var[par][:], vsum[par][:], 1.0 / C, EPS_LN, ALU.mult, ALU.add).then_inc(s_var, 1)
                if live(k + 1):
                    relation(k + 1, opp)
                if live(k):
                    ge(dve, pe_d, k - 1)
                    dve.wait_ge(s_rstd, k + 1)
                    dve.tensor_tensor(xn[par][:], xc[par][:].unsqueeze(2).broadcast_to([T, GB, 2, C]),
                                      rstd[par][:].unsqueeze(2).unsqueeze(3).broadcast_to([T, GB, 2, C]),
                                      ALU.mult).then_inc(s_xn, 1)


            def expert_step(k, par):
                opp = 1 - par
                if live(k):
                    ln_sum(k, par)
                if live(k - 2):
                    route_rest(k - 2, par)
                if live(k):
                    ln_mean(k, par)
                if live(k - 2):
                    route_top2(k - 2, par)
                if live(k - 3):
                    mix(k - 3, 0, opp)
                if live(k - 2):
                    route_equal2(k - 2, par)
                if live(k - 3):
                    mix_sum(k - 3, 0, opp)
                if live(k - 2):
                    route_rank2(k - 2, par)
                if live(k - 1):
                    x_high(k - 1, opp)
                if live(k - 2):
                    route_best2(k - 2, par)
                if live(k - 1):
                    x_low(k - 1, opp)
                if live(k - 2):
                    route_hot2(k - 2, par)
                if live(k - 3):
                    mix(k - 3, 1, opp)
                if live(k):
                    ln_square_sum(k, par)
                if live(k - 3):
                    mix_sum(k - 3, 1, opp)
                if live(k):
                    ln_variance(k, par)
                if live(k - 1):
                    route_logits(k - 1, opp)
                if live(k - 3):
                    mix(k - 3, 2, opp)
                if live(k - 1):
                    route_logits_sum(k - 1, opp)
                if live(k - 3):
                    mix_sum(k - 3, 2, opp)
                if live(k - 1):
                    route_top(k - 1, opp)
                if live(k):
                    ln_normalise(k, par)
                if live(k - 1):
                    route_equal(k - 1, opp)
                if live(k - 3):
                    mix(k - 3, 3, opp)
                if live(k - 1):
                    route_rank(k - 1, opp)
                if live(k - 3):
                    mix_sum(k - 3, 3, opp)
                if live(k - 1):
                    route_best(k - 1, opp)
                if live(k - 2):
                    dve.wait_ge(bpe_yb, k - 1)
                    ge(dve, b_final, k - 3)
                    dve.tensor_tensor(base[par][:], Wb[:, 0:GB * C].rearrange("p (b c) -> p b c", b=GB),
                                      resid[:, bass.ds((k - 2) * GB, GB), :], ALU.add).then_inc(b_base, 1)
                if live(k - 1):
                    route_hot(k - 1, opp)

            def handover():
                pass

            sweeps(dve, step, expert_step, handover)


def kernel(x, L0_tok_emb_table, L0_tok_W_in, L0_tok_b_oah, L0_attn_w_qkv, L0_attn_w_out, L0_attn_b_out,
           L0_ffn_gamma, L0_ffn_beta, L0_ffn_Wr, L0_ffn_br, L0_ffn_W1, L0_ffn_b1, L0_ffn_W2, L0_ffn_b2):
    import numpy as np
    import concourse.bacc as bacc
    from concourse.bass_utils import run_bass_kernel_spmd

    emb = np.asarray(L0_tok_emb_table)
    emb_ext = emb[(T - np.arange(2 * T)) % VROWS]
    arrays = {
        "x_ids": x, "emb_ext": emb_ext, "w_in_t": np.asarray(L0_tok_W_in).T, "b_oah": L0_tok_b_oah,
        "w_qkv": L0_attn_w_qkv, "w_out_t": np.asarray(L0_attn_w_out).T, "b_out": L0_attn_b_out,
        "gamma": L0_ffn_gamma, "beta": L0_ffn_beta, "w_r": L0_ffn_Wr, "b_r": L0_ffn_br,
        "w1": L0_ffn_W1, "b1_t": np.asarray(L0_ffn_b1).T, "w2": L0_ffn_W2, "b2": L0_ffn_b2,
    }
    arrays = {name: np.ascontiguousarray(a) for name, a in arrays.items()}
    nc = bacc.Bacc("TRN2", target_bir_lowering=False, num_devices=1)
    args = [nc.dram_tensor(name, a.shape, mybir.dt.from_np(a.dtype), kind="ExternalInput").ap()
            for name, a in arrays.items()]
    out = nc.dram_tensor("out", (B, T, C), F32, kind="ExternalOutput").ap()
    build_program(nc, *args, out)
    r = run_bass_kernel_spmd(nc, [arrays], core_ids=[0])
    return r.results[0]["out"]
```
